# Optimizing a Trainium2 kernel written in Bass

```python
import numpy as np
import jax
import jax.numpy as jnp

def _softmax(x, axis=-1):
    return jax.nn.softmax(x, axis=axis)

def _gelu(x):
    return jax.nn.gelu(x, approximate=True)

def _silu(x):
    return jax.nn.silu(x)

def _sigmoid(x):
    return jax.nn.sigmoid(x)

def _layernorm(x, axis=-1, eps=1e-05):
    m = jnp.mean(x, axis=axis, keepdims=True)
    v = jnp.var(x, axis=axis, keepdims=True)
    return (x - m) / jnp.sqrt(v + eps)

def _scatter_add(tgt, idx, src, axis=0):
    return tgt.at[idx].add(src)

def _segment_sum(src, seg, n):
    return jax.ops.segment_sum(src, seg, n)
kernel_name = 'mk_adaln_d1_jaxref_r8_6d238c'

def setup_inputs(seed: int=0):
    np.random.seed(seed)
    _w = jnp.asarray

    def _L0_attn_setup():
        import jax, jax.numpy as jnp
        import numpy as np
        B, T, IN_DIM, EMB = (8, 256, 128, 128)
        NEG_INF = -1e+30
        key = jax.random.key(seed)
        ks = jax.random.split(key, 7)
        s = 1.0 / np.sqrt(IN_DIM)
        return {'x': jax.random.normal(ks[0], (B, T, IN_DIM), dtype=jnp.float32), 'Wq': jax.random.normal(ks[1], (IN_DIM, EMB), dtype=jnp.float32) * s, 'bq': jax.random.normal(ks[2], (EMB,), dtype=jnp.float32) * 0.01, 'Wk': jax.random.normal(ks[3], (IN_DIM, EMB), dtype=jnp.float32) * s, 'bk': jax.random.normal(ks[4], (EMB,), dtype=jnp.float32) * 0.01, 'Wv': jax.random.normal(ks[5], (IN_DIM, EMB), dtype=jnp.float32) * s, 'bv': jax.random.normal(ks[6], (EMB,), dtype=jnp.float32) * 0.01}
    _L0_attn_in = _L0_attn_setup()

    def _L0_ffn_setup():
        import jax, jax.numpy as jnp
        import numpy as np
        DIM = 128
        DEPTH = 6
        HEADS = 16
        DIM_HEAD = 64
        WINDOW = 32
        INNER = HEADS * DIM_HEAD
        DIM_INNER = int(DIM * 4 * 2 / 3)
        QK_SCALE = 8.0

        def shift_tokens(t):
            a, s = jnp.split(t, 2, -1)
            s = jnp.pad(s, ((0, 0), (1, 0), (0, 0)))[:, :-1]
            return jnp.concatenate([a, s], -1)

        def l2norm(t):
            return t / jnp.maximum(jnp.linalg.norm(t, axis=-1, keepdims=True), 1e-12)

        def rotate_half(x):
            x1, x2 = jnp.split(x, 2, -1)
            return jnp.concatenate([-x2, x1], -1)

        def rotary_tables(n):
            half = jnp.arange(0, DIM_HEAD, 2, dtype=jnp.float32)
            inv_freq = 1.0 / 10000.0 ** (half / DIM_HEAD)
            t = jnp.arange(n, dtype=jnp.float32)
            freqs = t[:, None] * inv_freq[None, :]
            freqs = jnp.concatenate([freqs, freqs], -1)
            base_scale = (half + 0.4 * DIM_HEAD) / (1.4 * DIM_HEAD)
            power = (t - n // 2) / (WINDOW // 2)
            scale = base_scale[None, :] ** power[:, None]
            scale = jnp.concatenate([scale, scale], -1)
            return (freqs, scale)

        def local_attention(q, k, v):
            b, h, n, d = q.shape
            w = WINDOW
            nw = n // w
            bq = q.reshape(b, h, nw, w, d)
            bk = k.reshape(b, h, nw, w, d)
            bv = v.reshape(b, h, nw, w, d)

            def look(t):
                p = jnp.pad(t, ((0, 0), (0, 0), (1, 0), (0, 0), (0, 0)))
                return jnp.concatenate([p[:, :, :nw], p[:, :, 1:]], axis=3)
            bk2, bv2 = (look(bk), look(bv))
            seq = jnp.arange(n).reshape(nw, w)
            seq_p = jnp.pad(seq, ((1, 0), (0, 0)), constant_values=-1)
            jt = jnp.concatenate([seq_p[:nw], seq_p[1:]], axis=1)
            it = seq[:, :, None]
            jb = jt[:, None, :]
            mask = (it < jb) | (it > jb + w) | (jb == -1)
            sim = jnp.einsum('bhwie,bhwje->bhwij', bq, bk2) * QK_SCALE
            sim = jnp.where(mask, -jnp.finfo(sim.dtype).max, sim)
            attn = jax.nn.softmax(sim, -1)
            out = jnp.einsum('bhwij,bhwje->bhwie', attn, bv2)
            return out.reshape(b, h, n, d)

        def attn_layer(x, Wqkv, qs, ksc, Wo):
            b, n, _ = x.shape
            qkv = x @ Wqkv
            q, k, v = jnp.split(qkv, 3, -1)
            sh = lambda t: t.reshape(b, n, HEADS, DIM_HEAD).transpose(0, 2, 1, 3)
            q, k, v = (sh(q), sh(k), sh(v))
            q = l2norm(q) * qs
            k = l2norm(k) * ksc
            freqs, scale = rotary_tables(n)
            cos, sin = (jnp.cos(freqs), jnp.sin(freqs))
            q = q * cos * scale + rotate_half(q) * sin * scale
            inv = 1.0 / scale
            k = k * cos * inv + rotate_half(k) * sin * inv
            out = local_attention(q, k, v)
            out = out.transpose(0, 2, 1, 3).reshape(b, n, INNER)
            return out @ Wo

        def ffn_layer(x, g, bln, W1, b1, W2, b2):
            mu = x.mean(-1, keepdims=True)
            var = ((x - mu) ** 2).mean(-1, keepdims=True)
            xn = (x - mu) / jnp.sqrt(var + 1e-05) * g + bln
            hg = xn @ W1 + b1
            a, gate = jnp.split(hg, 2, -1)
            return a * jax.nn.gelu(gate, approximate=False) @ W2 + b2
        key = jax.random.key(seed)
        ks = jax.random.split(key, 8)
        B, N = (2, 256)
        init = lambda k, shape: jax.random.normal(k, shape, jnp.float32) * 0.02
        return {'x': jax.random.normal(ks[0], (B, N, DIM), jnp.float32), 'Wqkv': init(ks[1], (DEPTH, DIM, 3 * INNER)), 'q_scale': jnp.ones((DEPTH, DIM_HEAD), jnp.float32), 'k_scale': jnp.ones((DEPTH, DIM_HEAD), jnp.float32), 'Wo': init(ks[2], (DEPTH, INNER, DIM)), 'ln_g': jnp.ones((DEPTH, DIM), jnp.float32), 'ln_b': jnp.zeros((DEPTH, DIM), jnp.float32), 'W1': init(ks[3], (DEPTH, DIM, 2 * DIM_INNER)), 'b1': jnp.zeros((DEPTH, 2 * DIM_INNER), jnp.float32), 'W2': init(ks[4], (DEPTH, DIM_INNER, DIM)), 'b2': jnp.zeros((DEPTH, DIM), jnp.float32)}
    _L0_ffn_in = _L0_ffn_setup()
    _L0_c = _w((lambda *s: np.random.randn(*s).astype(np.float32) * 0.05)(1, 128))
    _L0_wmod = _w((lambda *s: np.random.randn(*s).astype(np.float32) * 0.05)(128, 6 * 128) * 128 ** (-0.5))
    _d = {'L0_attn_x': _L0_attn_in['x'], 'L0_attn_Wq': _L0_attn_in['Wq'], 'L0_attn_bq': _L0_attn_in['bq'], 'L0_attn_Wk': _L0_attn_in['Wk'], 'L0_attn_bk': _L0_attn_in['bk'], 'L0_attn_Wv': _L0_attn_in['Wv'], 'L0_attn_bv': _L0_attn_in['bv'], 'L0_ffn_Wqkv': _L0_ffn_in['Wqkv'], 'L0_ffn_q_scale': _L0_ffn_in['q_scale'], 'L0_ffn_k_scale': _L0_ffn_in['k_scale'], 'L0_ffn_Wo': _L0_ffn_in['Wo'], 'L0_ffn_ln_g': _L0_ffn_in['ln_g'], 'L0_ffn_ln_b': _L0_ffn_in['ln_b'], 'L0_ffn_W1': _L0_ffn_in['W1'], 'L0_ffn_b1': _L0_ffn_in['b1'], 'L0_ffn_W2': _L0_ffn_in['W2'], 'L0_ffn_b2': _L0_ffn_in['b2'], 'L0_c': _L0_c, 'L0_wmod': _L0_wmod}
    _x0 = _d['L0_attn_x']
    _d['L0_attn_x'] = jax.random.normal(jax.random.fold_in(jax.random.key(seed), 1), (1, 2048, 128), dtype=_x0.dtype)
    del _x0
    return _d

def reference(L0_attn_x, L0_attn_Wq, L0_attn_bq, L0_attn_Wk, L0_attn_bk, L0_attn_Wv, L0_attn_bv, L0_ffn_Wqkv, L0_ffn_q_scale, L0_ffn_k_scale, L0_ffn_Wo, L0_ffn_ln_g, L0_ffn_ln_b, L0_ffn_W1, L0_ffn_b1, L0_ffn_W2, L0_ffn_b2, L0_c, L0_wmod):

    def _L0_attn_ref(x, Wq, bq, Wk, bk, Wv, bv):
        import jax, jax.numpy as jnp
        import numpy as np
        B, T, IN_DIM, EMB = (8, 256, 128, 128)
        NEG_INF = -1e+30
        q = x @ Wq + bq
        k = x @ Wk + bk
        v = x @ Wv + bv
        scale = jnp.asarray(EMB, x.dtype) ** 0.5
        scores = jnp.einsum('btd,bsd->bts', q, k) / scale
        Tq = scores.shape[-2]
        causal = jnp.tril(jnp.ones((Tq, Tq), dtype=bool))
        scores = jnp.where(causal, scores, jnp.asarray(NEG_INF, scores.dtype))
        m = jnp.max(scores, axis=(-2, -1), keepdims=True)
        e = jnp.exp(scores - m)
        w = e / jnp.sum(e, axis=(-2, -1), keepdims=True)
        return jnp.einsum('bts,bsd->btd', w, v)

    def _L0_ffn_ref(x, Wqkv, q_scale, k_scale, Wo, ln_g, ln_b, W1, b1, W2, b2):
        import jax, jax.numpy as jnp
        import numpy as np
        DIM = 128
        DEPTH = 6
        HEADS = 16
        DIM_HEAD = 64
        WINDOW = 32
        INNER = HEADS * DIM_HEAD
        DIM_INNER = int(DIM * 4 * 2 / 3)
        QK_SCALE = 8.0

        def shift_tokens(t):
            a, s = jnp.split(t, 2, -1)
            s = jnp.pad(s, ((0, 0), (1, 0), (0, 0)))[:, :-1]
            return jnp.concatenate([a, s], -1)

        def l2norm(t):
            return t / jnp.maximum(jnp.linalg.norm(t, axis=-1, keepdims=True), 1e-12)

        def rotate_half(x):
            x1, x2 = jnp.split(x, 2, -1)
            return jnp.concatenate([-x2, x1], -1)

        def rotary_tables(n):
            half = jnp.arange(0, DIM_HEAD, 2, dtype=jnp.float32)
            inv_freq = 1.0 / 10000.0 ** (half / DIM_HEAD)
            t = jnp.arange(n, dtype=jnp.float32)
            freqs = t[:, None] * inv_freq[None, :]
            freqs = jnp.concatenate([freqs, freqs], -1)
            base_scale = (half + 0.4 * DIM_HEAD) / (1.4 * DIM_HEAD)
            power = (t - n // 2) / (WINDOW // 2)
            scale = base_scale[None, :] ** power[:, None]
            scale = jnp.concatenate([scale, scale], -1)
            return (freqs, scale)

        def local_attention(q, k, v):
            b, h, n, d = q.shape
            w = WINDOW
            nw = n // w
            bq = q.reshape(b, h, nw, w, d)
            bk = k.reshape(b, h, nw, w, d)
            bv = v.reshape(b, h, nw, w, d)

            def look(t):
                p = jnp.pad(t, ((0, 0), (0, 0), (1, 0), (0, 0), (0, 0)))
                return jnp.concatenate([p[:, :, :nw], p[:, :, 1:]], axis=3)
            bk2, bv2 = (look(bk), look(bv))
            seq = jnp.arange(n).reshape(nw, w)
            seq_p = jnp.pad(seq, ((1, 0), (0, 0)), constant_values=-1)
            jt = jnp.concatenate([seq_p[:nw], seq_p[1:]], axis=1)
            it = seq[:, :, None]
            jb = jt[:, None, :]
            mask = (it < jb) | (it > jb + w) | (jb == -1)
            sim = jnp.einsum('bhwie,bhwje->bhwij', bq, bk2) * QK_SCALE
            sim = jnp.where(mask, -jnp.finfo(sim.dtype).max, sim)
            attn = jax.nn.softmax(sim, -1)
            out = jnp.einsum('bhwij,bhwje->bhwie', attn, bv2)
            return out.reshape(b, h, n, d)

        def attn_layer(x, Wqkv, qs, ksc, Wo):
            b, n, _ = x.shape
            qkv = x @ Wqkv
            q, k, v = jnp.split(qkv, 3, -1)
            sh = lambda t: t.reshape(b, n, HEADS, DIM_HEAD).transpose(0, 2, 1, 3)
            q, k, v = (sh(q), sh(k), sh(v))
            q = l2norm(q) * qs
            k = l2norm(k) * ksc
            freqs, scale = rotary_tables(n)
            cos, sin = (jnp.cos(freqs), jnp.sin(freqs))
            q = q * cos * scale + rotate_half(q) * sin * scale
            inv = 1.0 / scale
            k = k * cos * inv + rotate_half(k) * sin * inv
            out = local_attention(q, k, v)
            out = out.transpose(0, 2, 1, 3).reshape(b, n, INNER)
            return out @ Wo

        def ffn_layer(x, g, bln, W1, b1, W2, b2):
            mu = x.mean(-1, keepdims=True)
            var = ((x - mu) ** 2).mean(-1, keepdims=True)
            xn = (x - mu) / jnp.sqrt(var + 1e-05) * g + bln
            hg = xn @ W1 + b1
            a, gate = jnp.split(hg, 2, -1)
            return a * jax.nn.gelu(gate, approximate=False) @ W2 + b2
        for i in range(DEPTH):
            x = attn_layer(shift_tokens(x), Wqkv[i], q_scale[i], k_scale[i], Wo[i]) + x
            x = ffn_layer(shift_tokens(x), ln_g[i], ln_b[i], W1[i], b1[i], W2[i], b2[i]) + x
        return x
    x = L0_attn_x
    mod = (_silu(L0_c) @ L0_wmod).reshape(L0_c.shape[0], 6, 1, -1)
    sa, ca, ga, sb, cb, gb = (mod[:, 0], mod[:, 1], mod[:, 2], mod[:, 3], mod[:, 4], mod[:, 5])
    ga = (2 * (ga >= 0) - 1) * jnp.maximum(jnp.abs(ga), 0.25)
    gb = (2 * (gb >= 0) - 1) * jnp.maximum(jnp.abs(gb), 0.25)
    h = _layernorm(x, axis=-1) * (1 + ca) + sa
    x = x + ga * _L0_attn_ref(h, L0_attn_Wq, L0_attn_bq, L0_attn_Wk, L0_attn_bk, L0_attn_Wv, L0_attn_bv)
    h = _layernorm(x, axis=-1) * (1 + cb) + sb
    x = x + gb * _L0_ffn_ref(h, L0_ffn_Wqkv, L0_ffn_q_scale, L0_ffn_k_scale, L0_ffn_Wo, L0_ffn_ln_g, L0_ffn_ln_b, L0_ffn_W1, L0_ffn_b1, L0_ffn_W2, L0_ffn_b2)
    return x

_drawn_inputs = setup_inputs


def setup_inputs(seed=0):
    import zlib

    import numpy as np

    out = dict(_drawn_inputs(seed))
    spreads = {'L0_ffn_q_scale': (1.0, 0.6),
     'L0_ffn_k_scale': (1.0, 0.6),
     'L0_ffn_ln_g': (1.0, 0.6),
     'L0_ffn_ln_b': (0.0, 0.8),
     'L0_ffn_b1': (0.0, 0.8),
     'L0_ffn_b2': (0.0, 0.607)}
    factors = {'L0_attn_Wq': 8.0,
     'L0_attn_bq': 8.0,
     'L0_attn_Wk': 8.0,
     'L0_attn_bk': 8.0,
     'L0_attn_Wv': 22.38,
     'L0_attn_bv': 64.0,
     'L0_ffn_W1': 7.218,
     'L0_ffn_W2': 7.084}
    for name, (base, spread) in spreads.items():
        noise = np.random.default_rng([zlib.crc32(name.encode()), seed]).standard_normal(out[name].shape)
        drawn = base * np.exp(spread * noise) if base else spread * noise
        out[name] = jnp.asarray(drawn.astype(out[name].dtype))
    for name, factor in factors.items():
        out[name] = (out[name] * factor).astype(out[name].dtype)
    return out
```

```python
from contextlib import ExitStack

import numpy as np

import concourse.bass as bass
from concourse import mybir

F32 = mybir.dt.float32
I32 = mybir.dt.int32
ALU = mybir.AluOpType
ACT = mybir.ActivationFunctionType
AX = mybir.AxisListType

P = 128
T = 2048
NT = T // P
L = 6
H = 16
DH = 64
W = 32
NW = P // W
PR = H // 2
NK = 2 * W
FI = 341
FCH = [(0, 128), (128, 128), (256, 85)]
E = L * NT
BANK = 512
BIG = 1.0e30
MAGIC = 0x5F3759DF
LN_EPS = 1e-5
NORM_EPS2 = 1e-24
FILL, UNROLL = 6, 2
LAST = E + 5


def shape_tables():
    f = np.float32
    half = np.arange(0, DH, 2, dtype=f)
    inv = (f(1.0) / np.power(f(10000.0), half / f(DH))).astype(f)
    t = np.arange(T, dtype=f)
    fr = (t[:, None] * inv[None, :]).astype(f)
    fr = np.concatenate([fr, fr], -1)
    base = (half.astype(np.float64) + 0.4 * DH) / (1.4 * DH)
    sc = base[None, :] ** ((np.arange(T) % P - P // 2) / (W // 2))[:, None]
    sc = np.concatenate([sc, sc], -1)
    carry = np.tile(base ** (P / (W // 2)), P // len(base))[:, None]
    cos, sin = np.cos(fr).astype(f), np.sin(fr).astype(f)
    sgn = np.concatenate([-np.ones(DH // 2, f), np.ones(DH // 2, f)])
    iv = 1.0 / sc
    tab = np.stack([cos * sc, sin * sgn * sc, cos * iv, sin * sgn * iv], 1).astype(f)
    tab = tab.reshape(NT, P, 4 * DH).transpose(1, 0, 2).reshape(P, NT * 4 * DH)
    q = np.arange(P)
    i, j = (q % W)[:, None], np.arange(NK)[None, :]
    m = np.where((j >= i) & (j <= i + W), 0.0, -BIG)
    mask = np.repeat(m[:, None, :], NT, 1)
    mask[:W, 0, :W] = -BIG
    diag = np.where(q[None, :] >= q[:, None], 0.0, -BIG)
    return [np.ascontiguousarray(a, f) for a in (np.eye(P), tab, mask.reshape(P, NT * NK), diag, carry)]


def program(nc, x, wq, bq, wk, bk, wv, bv, wqkv, qs, ks, wo, lng, lnb, w1, b1, w2, b2, c, wmod,
            eye, tab, maskt, diagt, carryt, out):
    SCALE = float(P) ** -0.5
    ctx = ExitStack()
    with ctx:
        def sb(name, *shape, dt=F32):
            return ctx.enter_context(nc.sbuf_tensor(name, [P, *shape], dt))

        def sem(name):
            return ctx.enter_context(nc.semaphore(name))

        ident = sb("ident", P)
        diag = sb("diag", P)
        maskb = sb("maskb", NT * NK)
        tabb = sb("tabb", NT * 4 * DH)
        wqk = sb("wqk", 2 * 2048)
        w1b = sb("w1b", 2 * 2 * FI)
        b1b = sb("b1b", 2 * 2 * FI)
        w2b = sb("w2b", 2 * 3 * P)
        scl = sb("scl", 2 * 4 * DH)
        wvo = sb("wvo", L * H * P)
        PAD = W + 1
        xa = sb("xa", PAD + T)
        xb = sb("xb", 1 + T)
        x1 = sb("x1", T)
        vtok = sb("vtok", T)
        arena = sb("arena", 136 * P)
        small = sb("small", 1024)
        at = [0]

        def cols(n):
            at[0] += n
            return small[:, at[0] - n:at[0]]

        ccol, sig, silu = cols(1), cols(1), cols(1)
        modT, ca1, cb1, gaf, gbf, tmpa, tmpb = cols(6), cols(1), cols(1), cols(1), cols(1), cols(2), cols(2)
        bqc, bkc = cols(1), cols(1)
        bvr = cols(P)
        bnst, bnmv, rs16 = cols(6 * NT), cols(2 * NT), cols(NT)
        mx, negm, esum, gs, zc, zr, mcol = cols(NT), cols(NT), cols(NT), cols(NT), cols(1), cols(1), cols(1)
        mrow, ones = cols(P), cols(P)
        lngT, lnbT, b2T = cols(L), cols(L), cols(L)
        nw_x, nw_y, nw_a, nw_b = cols(33), cols(33), cols(33), cols(33)
        ri_, carry = cols(16), cols(1)
        st2, mv2 = cols(6), cols(2)
        rk = [cols(33), cols(33)]
        q8 = [cols(16), cols(16)]
        smax, nbias, rsum = cols(16), cols(16), cols(16)

        wmod_s = arena[:, 0:768]
        wq_s, wk_s, wv_s = arena[:, 768:896], arena[:, 896:1024], arena[:, 1024:1152]
        xtok = arena[:, 2048:4096].rearrange("p (t d) -> p t d", t=NT)
        xntok = arena[:, 4096:6144].rearrange("p (t d) -> p t d", t=NT)
        wv_st = [arena[:, 6144 + 1024 * i:7168 + 1024 * i] for i in range(2)]
        wo_st = [arena[:, 8192 + 1024 * i:9216 + 1024 * i] for i in range(2)]
        wvT = arena[:, 10240:11264]
        hT, qT0, kT0 = xa[:, 0:T], xb[:, 0:T], wqk[:, 2048:4096]
        eoff = [0]
        for s in range(NT):
            eoff.append(eoff[-1] + T - P * s)

        off = [0]

        def buf(n):
            off[0] += n
            return arena[:, off[0] - n:off[0]]

        xs = [buf(P + W), buf(P + W)]
        xd = buf(NW * 2 * NK)
        xw = [buf(NW * P), buf(NW * P)]
        tabs = [buf(4 * DH), buf(4 * DH)]
        sqq, sqk = buf(1024), buf(1024)
        qc, qsn, kc, ksn = buf(1024), buf(1024), buf(1024), buf(1024)
        QT, KT = buf(1024), buf(PR * (P + W))
        sm, pr, pT = buf(1024), buf(1024), buf(1024)
        ysb = [buf(1024), buf(1024)]
        osb, xs2, xn2, xnT, x2c = buf(P), buf(P), buf(P), buf(P), buf(P)
        gate, gel, ha, hh = (vtok[:, FI * i:FI * i + FI] for i in range(4))
        hT_, fsb = vtok[:, 4 * FI:4 * FI + 3 * P], vtok[:, 4 * FI + 3 * P:4 * FI + 4 * P]
        QT3 = QT.rearrange("p (a t) -> p a t", a=PR)
        KT3 = KT.rearrange("p (a t) -> p a t", a=PR)
        pT3 = pT.rearrange("p (a t) -> p a t", a=PR)

        ps = ctx.enter_context(nc.psum_tensor("ps", [P, 8 * BANK], F32))
        pj = ps[:, 0:1024]
        tp = ps[:, 1024:2048]
        sy = ps[:, 2048:3072]
        b6 = ps[:, 3072:3584]
        b7 = ps[:, 3584:4096]

        s_x, s_cw, s_wl, s_small = sem("s_x"), sem("s_cw"), sem("s_wl"), sem("s_small")
        s_id, s_wqk, s_w1, s_b1, s_w2 = sem("s_id"), sem("s_wqk"), sem("s_w1"), sem("s_b1"), sem("s_w2")
        s_scl, s_tab, s_msk, s_lnp = sem("s_scl"), sem("s_tab"), sem("s_msk"), sem("s_lnp")
        s_wst = [sem("s_wst0"), sem("s_wst1")]
        s_out = sem("s_out")
        v_ch = sem("v_ch")
        a_sig, v_silu, t_mod, v_mod = sem("a_sig"), sem("v_silu"), sem("t_mod"), sem("v_mod")
        v_xn, t_xT, t_xnT, a_x1, a_hT = sem("v_xn"), sem("t_xT"), sem("t_xnT"), sem("a_x1"), sem("a_hT")
        t_q, t_k, t_v, a_qk, v_v = sem("t_q"), sem("t_k"), sem("t_v"), sem("a_qk"), sem("v_v")
        t_wvT, a_wvT, t_m, a_m = sem("t_wvT"), sem("a_wvT"), sem("t_m"), sem("a_m")
        t_s, v_nm, a_e = sem("t_s"), sem("v_nm"), sem("a_e")
        t_mr, v_mrow, t_mc, v_mcol, a_gs, v_z, t_z, v_vs = (sem("t_mr"), sem("v_mrow"), sem("t_mc"), sem("v_mcol"),
                                                    sem("a_gs"), sem("v_z"), sem("t_z"), sem("v_vs"))
        t_av, v_x1, t_x1t, v_xn2, t_x2T, a_xa = (sem("t_av"), sem("v_x1"), sem("t_x1t"), sem("v_xn2"),
                                                 sem("t_x2T"), sem("a_xa"))
        g_init = sem("g_init")
        v_fin, t_fin, a_fin = sem("v_fin"), sem("t_fin"), sem("a_fin")
        names = ("g_xs g_xd g_tab g_qr g_kr g_krn g_pn g_xs2 g_kcar "
                 "t_tq t_tk t_xw t_pq t_pk t_sc t_pT t_y0 t_y1 t_o t_to t_x2 t_xnt t_hg t_ha t_th t_w2 t_tf "
                 "a_sqq a_sqk a_QT a_KT a_ex a_pT a_y0 a_y1 a_gel "
                 "v_xw v_f v_xb v_qq v_xa v_xnT v_ssq v_ms v_nb v_bn v_kk v_ssk v_gate v_ha v_rs v_mx v_lnx v_h v_os v_hT v_ri")
        S = {n: sem("p" + n) for n in names.split()}

        block = ctx.enter_context(nc.Block())

        def need(eng, name, e):
            if isinstance(e, int):
                e = min(e, E - 1)
                if e + ahead.get(name, 0) < 0:
                    return
            eng.wait_ge(S[name], e + (ahead.get(name, 0) + 1))

        ahead = {"v_xa": NT}

        def apart(eng):
            eng.wait_ge(s_id, 16)

        def live(e):
            return not isinstance(e, int) or 0 <= e < E

        def run(eng, step, end=E):
            for n in range(FILL):
                step(n, n % 2)
            with eng.Fori(FILL, end, UNROLL) as i:
                for u in range(UNROLL):
                    step(i + u, u)
            for n in range(end, LAST):
                step(n, n % 2)

        def tile_of(e):
            return e % NT

        def layer_of(e):
            return e // NT

        def slot_of(e):
            return (e // NT) % 2

        @block.sync
        def _(sp):
            sp.dma_start(xtok, x[0].rearrange("(t p) d -> p t d", p=P)).then_inc(s_x, 16)
            sp.dma_start(ident[:, :], eye).then_inc(s_id, 16)
            sp.dma_start(ccol, c).then_inc(s_cw, 16)
            sp.dma_start(wmod_s, wmod).then_inc(s_cw, 16)
            sp.dma_start(wq_s, wq).then_inc(s_wl, 16)
            sp.dma_start(wk_s, wk).then_inc(s_wl, 16)
            sp.dma_start(wv_s, wv).then_inc(s_wl, 16)
            sp.dma_start(bqc, bq.rearrange("(d a) -> d a", a=1)).then_inc(s_wl, 16)
            sp.dma_start(bkc, bk.rearrange("(d a) -> d a", a=1)).then_inc(s_wl, 16)
            sp.dma_start(bvr, bv.partition_broadcast(P)).then_inc(s_wl, 16)
            sp.dma_start(diag[:, :], diagt).then_inc(s_wl, 16)
            for l in range(L):
                if l >= 2:
                    sp.wait_ge(t_m, l - 1)
                sp.dma_start(wv_st[l % 2], wqkv[l, :, 2048:3072]).then_inc(s_wst[l % 2], 16)
                sp.dma_start(wo_st[l % 2].rearrange("p (a d) -> p a d", a=PR),
                             wo[l].rearrange("(a p) d -> p a d", p=P)).then_inc(s_wst[l % 2], 16)
            sp.dma_start(maskb[:, :], maskt).then_inc(s_msk, 16)
            sp.dma_start(tabb[:, :], tab).then_inc(s_tab, 16)
            sp.dma_start(carry, carryt).then_inc(s_lnp, 16)
            sp.dma_start(lngT, lng).then_inc(s_lnp, 16)
            sp.dma_start(lnbT, lnb).then_inc(s_lnp, 16)
            sp.dma_start(b2T, b2).then_inc(s_lnp, 16)

            def layer_weights(l):
                o = (l % 2)
                def dst(t, n):
                    return t[:, bass.ds(o * n, n)]
                sp.dma_start(dst(wqk, 2048), wqkv[l, :, 0:2048]).then_inc(s_wqk, 16)
                sp.dma_start(dst(w1b, 2 * FI), w1[l]).then_inc(s_w1, 16)
                sp.dma_start(dst(b1b, 2 * FI), b1[l].partition_broadcast(P)).then_inc(s_b1, 16)
                w2d = dst(w2b, 3 * P)
                for j, (k0, kn) in enumerate(FCH):
                    sp.dma_start(w2d[0:kn, j * P:(j + 1) * P], w2[l, k0:k0 + kn, :]).then_inc(s_w2, 16)
                for j, (r, lo) in enumerate(((qs, 0), (qs, 1), (ks, 0), (ks, 1))):
                    sd = dst(scl, 4 * DH)
                    if lo == 0:
                        sp.dma_start(sd[:, j * DH:(j + 1) * DH], r[l].partition_broadcast(P)).then_inc(s_scl, 16)
                    else:
                        for a in range(2):
                            sp.dma_start(sd[:, j * DH + 32 * a:j * DH + 32 * a + 32],
                                         r[l, 32 - 32 * a:64 - 32 * a].partition_broadcast(P)).then_inc(s_scl, 16)

            layer_weights(0)
            sp.wait_ge(t_s, NT)
            for s_, v_ in ((s_wqk, 16), (s_w1, 16), (s_b1, 16), (s_w2, 48), (s_scl, 96)):
                sp.wait_ge(s_, v_)
            layer_weights(1)
            with sp.Fori(2, L) as l:
                through = sp.snap(l * NT - (NT - 1))
                apart(sp)
                sp.wait_ge(S["t_w2"], through)
                layer_weights(l)
            for i in range(4):
                sp.wait_ge(a_fin, i + 1)
                sp.dma_start(out[0, 512 * i:512 * i + 512].rearrange("(t p) d -> p t d", p=P),
                             xtok[:, 4 * i:4 * i + 4, :]).then_inc(s_out, 16)
            sp.wait_ge(s_out, 64)

        @block.tensor
        def _(pe):
            mm = nc.tensor.matmul

            def tr(o, i, n=P):
                return nc.tensor.transpose(o, i, ident[0:n, 0:n])

            pe.wait_ge(s_cw, 32)
            pe.wait_ge(v_silu, 1)
            for j in range(6):
                last = mm(b7[:, j:j + 1], wmod_s[:, j * P:(j + 1) * P], silu, start=True, stop=True)
            last.then_inc(t_mod, 1)
            pe.wait_ge(s_x, 16)
            pe.wait_ge(s_id, 16)
            for t in range(NT):
                last = tr(ps[:, P * t:P * t + P], xtok[:, t, :])
                if t % 4 == 3:
                    last.then_inc(t_xT, 1)
            pe.wait_ge(v_mod, 1)
            for t in range(NT):
                if t % 4 == 0:
                    pe.wait_ge(v_xn, t + 4)
                last = tr(ps[:, T + P * t:T + P * t + P], xntok[:, t, :])
                if t % 4 == 3:
                    last.then_inc(t_xnT, 1)
            pe.wait_ge(s_wl, 112)
            for j in range(4):
                pe.wait_ge(a_x1, j + 1)
                pe.wait_ge(a_hT, j + 1)
                mm(ps[:, 512 * j:512 * j + 512], wq_s, hT[:, 512 * j:512 * j + 512],
                   start=True, stop=True).then_inc(t_q, 1)
            for j in range(4):
                mm(ps[:, T + 512 * j:T + 512 * j + 512], wk_s, hT[:, 512 * j:512 * j + 512],
                   start=True, stop=True).then_inc(t_k, 1)
            for t in range(NT):
                if t % 4 == 0:
                    pe.wait_ge(a_qk, t // 4 + 1)
                last = mm(ps[:, P * t:P * t + P], hT[:, P * t:P * t + P], wv_s, start=True, stop=True)
                if t % 4 == 3:
                    last.then_inc(t_v, 1)
            for l in range(L):
                pe.wait_ge(s_wst[l % 2], 32 * (l // 2 + 1))
                if l == 0:
                    pe.wait_ge(v_v, 2)
                    pe.wait_ge(a_qk, 8)
                else:
                    pe.wait_ge(a_wvT, l)
                for p in range(PR):
                    last = tr(ps[:, P * p:P * p + P], wv_st[l % 2][:, P * p:P * p + P])
                last.then_inc(t_wvT, 1)
                pe.wait_ge(a_wvT, l + 1)
                if l:
                    pe.wait_ge(a_m, l)
                for p in range(PR):
                    for r in range(2):
                        last = mm(ps[:, T + 1024 * r + P * p:T + 1024 * r + P * p + P],
                                  wvT[DH * r:DH * r + DH, P * p:P * p + P],
                                  wo_st[l % 2][DH * r:DH * r + DH, P * p:P * p + P], start=True, stop=True)
                last.then_inc(t_m, 1)
            pe.wait_ge(v_v, 4)
            pe.wait_ge(a_m, L)
            for s in range(NT):
                base = T * (s % 2)
                if s >= 2:
                    pe.wait_ge(a_e, s - 1)
                for j in range(s // 4, 4):
                    lo = max(512 * j, P * s)
                    last = mm(ps[:, base + lo:base + 512 * j + 512], kT0[:, P * s:P * s + P],
                              qT0[:, lo:512 * j + 512], start=True, stop=True)
                last.then_inc(t_s, 1)
            pe.wait_ge(v_mrow, 1)
            tr(ps[0:1, 0:P], mcol).then_inc(t_mr, 1)
            pe.wait_ge(v_mrow, 2)
            mm(ps[:, 512:513], ones[0:1, :], mrow[0:1, 0:1], start=True, stop=True).then_inc(t_mc, 1)
            pe.wait_ge(v_z, 1)
            mm(ps[:, 1024:1025], ones, zc, start=True, stop=True).then_inc(t_z, 1)
            pe.wait_ge(v_vs, 1)
            for j in range(4):
                for s in range(4 * j + 4):
                    lo = max(512 * j, P * s)
                    last = mm(ps[:, lo:512 * j + 512], vtok[:, P * s:P * s + P],
                              arena[:, eoff[s] + lo - P * s:eoff[s] + 512 * j + 512 - P * s],
                              start=(s == 0), stop=(s == 4 * j + 3))
                last.then_inc(t_av, 1)
            for j in range(4):
                pe.wait_ge(v_x1, j + 1)
                for t in range(4 * j, 4 * j + 4):
                    last = tr(ps[:, T + P * t:T + P * t + P], x1[:, P * t:P * t + P])
                last.then_inc(t_x1t, 1)
            for j in range(4):
                pe.wait_ge(v_xn2, 4 * j + 4)
                for t in range(4 * j, 4 * j + 4):
                    last = tr(ps[:, P * t:P * t + P], xntok[:, t, :])
                last.then_inc(t_x2T, 1)

            def step(n, u):
                if live(n - 1):
                    need(pe, "g_qr", n - 1)
                    need(pe, "a_y1", n - 3)
                    for p in range(PR):
                        last = tr(tp[:, P * p:P * p + P], qc[:, P * p:P * p + P])
                    last.then_inc(S["t_tq"], 1)
                if live(n - 1):
                    need(pe, "g_xd", n - 1)
                    need(pe, "v_os", n - 3)
                    for j in range(NW):
                        last = tr(b7[:, P * j:P * j + P], xd[:, P * j:P * j + P])
                    last.then_inc(S["t_xw"], 1)
                if live(n - 5):
                    need(pe, "v_h", n - 5)
                    for j, (k0, kn) in enumerate(FCH):
                        last = tr(b6[0:kn, P * j:P * j + P], hh[:, k0:k0 + kn])
                    last.then_inc(S["t_th"], 1)

                if live(n):
                    need(pe, "g_xs", n)
                    need(pe, "a_sqk", n - 1)
                    need(pe, "v_kk", n - 1)
                    pe.wait_ge(s_wqk, (layer_of(n) + 1) * 16)
                    for j in range(2):
                        last = mm(pj[:, 512 * j:512 * j + 512], xs[u][:, W:],
                                  wqk[:, bass.ds(slot_of(n) * 2048 + 512 * j, 512)], start=True, stop=True)
                    last.then_inc(S["t_pq"], 1)
                if live(n - 1):
                    need(pe, "g_krn", n - 1)
                    need(pe, "a_QT", n - 1)
                    for p in range(PR):
                        last = tr(tp[:, P * p:P * p + P], kc[:, P * p:P * p + P])
                    last.then_inc(S["t_tk"], 1)
                if live(n - 3):
                    need(pe, "v_os", n - 3)
                    need(pe, "v_xw", n - 1)
                    tr(b7[:, 0:P], osb).then_inc(S["t_to"], 1)
                if live(n - 5):
                    need(pe, "v_hT", n - 5)
                    pe.wait_ge(s_w2, (layer_of(n - 5) + 1) * 48)
                    for j, (k0, kn) in enumerate(FCH):
                        last = mm(b6[:, 384:512], hT_[0:kn, P * j:P * j + P],
                                  w2b[0:kn, bass.ds(slot_of(n - 5) * 3 * P + P * j, P)],
                                  start=(j == 0), stop=(j == 2))
                    last.then_inc(S["t_w2"], 1)
                if live(n - 4):
                    need(pe, "v_lnx", n - 4)
                    need(pe, "v_xb", n - 3)
                    tr(b7[:, P:2 * P], xn2).then_inc(S["t_xnt"], 1)
                if live(n - 1):
                    apart(pe)
                    need(pe, "a_KT", n - 1)
                    need(pe, "g_kcar", n - 1)
                    need(pe, "a_y0", n - 3)
                    for p in range(PR):
                        for r in range(2):
                            for j in range(NW):
                                last = mm(sy[W * j:W * j + W, 512 * r + NK * p:512 * r + NK * p + NK],
                                          QT3[DH * r:DH * r + DH, p, W * j:W * j + W],
                                          KT3[DH * r:DH * r + DH, p, W * j:W * j + NK], start=True, stop=True)
                    last.then_inc(S["t_sc"], 1)
                if live(n - 5):
                    need(pe, "v_f", n - 5)
                    tr(b6[:, 0:P], fsb).then_inc(S["t_tf"], 1)
                if live(n):
                    need(pe, "a_sqq", n)
                    need(pe, "v_qq", n)
                    for j in range(2):
                        last = mm(pj[:, 512 * j:512 * j + 512], xs[u][:, W:],
                                  wqk[:, bass.ds(slot_of(n) * 2048 + 1024 + 512 * j, 512)],
                                  start=True, stop=True)
                    last.then_inc(S["t_pk"], 1)
                if live(n - 2):
                    need(pe, "g_pn", n - 2)
                    need(pe, "a_KT", n - 1)
                    for p in range(PR):
                        last = tr(tp[:, P * p:P * p + P], pr[:, P * p:P * p + P])
                    last.then_inc(S["t_pT"], 1)
                if live(n - 3):
                    need(pe, "g_xs2", n - 3)
                    need(pe, "v_xa", n - 5)
                    tr(b6[:, 0:P], xs2).then_inc(S["t_x2"], 1)
                if live(n - 4):
                    need(pe, "v_xnT", n - 4)
                    need(pe, "v_bn", n - 3)
                    need(pe, "v_xa", n - 5)
                    pe.wait_ge(s_w1, (layer_of(n - 4) + 1) * 16)
                    mm(b6[:, 0:FI], xnT, w1b[:, bass.ds(slot_of(n - 4) * 2 * FI + FI, FI)],
                       start=True, stop=True).then_inc(S["t_hg"], 1)

                def values(r, name, o):
                    for j in range(NW):
                        last = mm(o[:, 256 * j:256 * j + 256].rearrange("p (a q) -> p a q", a=PR),
                                  xw[u][DH * r:DH * r + DH, P * j:P * j + P],
                                  pT3[DH * r:DH * r + DH, :, W * j:W * j + W], start=True, stop=True)
                    last.then_inc(S[name], 1)

                if live(n - 2):
                    need(pe, "a_pT", n - 2)
                    need(pe, "v_xw", n - 2)
                    need(pe, "v_ms", n - 1)
                    values(0, "t_y0", sy)
                if live(n - 4):
                    need(pe, "v_gate", n - 4)
                    mm(b6[:, 0:FI], xnT, w1b[:, bass.ds(slot_of(n - 4) * 2 * FI, FI)],
                       start=True, stop=True).then_inc(S["t_ha"], 1)
                if live(n - 2):
                    values(1, "t_y1", tp)
                    need(pe, "v_xb", n - 3)
                    need(pe, "v_xnT", n - 4)
                    for r in range(2):
                        need(pe, "a_y0" if r == 0 else "a_y1", n - 2)
                        for p in range(PR):
                            last = mm(b7[:, 0:P],
                                      ysb[r][:, P * p:P * p + P],
                                      wvo[:, bass.ds(layer_of(n - 2) * (H * P) + (r * PR + p) * P, P)],
                                      start=(r == 0 and p == 0), stop=(r == 1 and p == PR - 1))
                    last.then_inc(S["t_o"], 1)
            pe.wait_ge(a_xa, 4)
            pe.wait_ge(g_init, 3)
            run(pe, step)

            for i in range(4):
                pe.wait_ge(v_fin, i + 1)
                for t in range(4 * i, 4 * i + 4):
                    last = tr(ps[:, P * t:P * t + P], x1[:, P * t:P * t + P])
                last.then_inc(t_fin, 1)

        @block.scalar
        def _(act):
            A = nc.scalar.activation

            def heads_first(ap):
                return ap.rearrange("d (a j q) -> d j a q", j=NW, a=PR)

            def by_window(ap):
                return ap.rearrange("d (j a q) -> d j a q", j=NW, a=PR)

            act.wait_ge(s_cw, 32)
            A(sig, ccol, ACT.Exp, scale=-1.0).then_inc(a_sig, 1)
            for j in range(4):
                act.wait_ge(t_xT, j + 1)
                A(x1[:, 512 * j:512 * j + 512], ps[:, 512 * j:512 * j + 512], ACT.Copy).then_inc(a_x1, 1)
            act.wait_ge(v_mod, 1)
            for j in range(4):
                act.wait_ge(t_xnT, j + 1)
                A(hT[:, 512 * j:512 * j + 512], ps[:, T + 512 * j:T + 512 * j + 512], ACT.Identity,
                  scale=ca1, bias=modT[:, 0:1]).then_inc(a_hT, 1)
            act.wait_ge(s_wl, 112)
            for j in range(4):
                act.wait_ge(t_q, j + 1)
                A(qT0[:, 512 * j:512 * j + 512], ps[:, 512 * j:512 * j + 512], ACT.Identity,
                  bias=bqc).then_inc(a_qk, 1)
            for j in range(4):
                act.wait_ge(t_k, j + 1)
                A(kT0[:, 512 * j:512 * j + 512], ps[:, T + 512 * j:T + 512 * j + 512], ACT.Identity,
                  bias=bkc).then_inc(a_qk, 1)
            for l in range(L):
                act.wait_ge(t_wvT, l + 1)
                if l:
                    act.wait_ge(t_m, l)
                A(wvT, ps[:, 0:1024], ACT.Copy).then_inc(a_wvT, 1)
                act.wait_ge(t_m, l + 1)
                A(wvo[:, l * H * P:(l + 1) * H * P], ps[:, T:T + H * P], ACT.Copy).then_inc(a_m, 1)
            act.wait_ge(v_v, 4)
            for s in range(NT):
                act.wait_ge(v_nm, s + 1)
                base = T * (s % 2)
                A(arena[:, eoff[s]:eoff[s + 1]], ps[:, base + P * s:base + T], ACT.Exp,
                  scale=SCALE, bias=negm[:, s:s + 1], accum_out=esum[:, s:s + 1]).then_inc(a_e, 1)
            act.wait_ge(v_mcol, 1)
            A(gs, mx, ACT.Exp, scale=SCALE, bias=mcol).then_inc(a_gs, 1)
            act.wait_ge(g_init, 3)
            for j in range(4):
                act.wait_ge(t_x2T, j + 1)
                A(xa[:, PAD + 512 * j:PAD + 512 * j + 512], ps[:, 512 * j:512 * j + 512], ACT.Identity,
                  scale=cb1, bias=modT[:, 3:4]).then_inc(a_xa, 1)

            def step(n, u):
                if live(n - 1):
                    need(act, "t_tq", n - 1)
                    need(act, "t_sc", n - 2)
                    A(QT, tp, ACT.Copy).then_inc(S["a_QT"], 1)
                if live(n):
                    need(act, "t_pq", n)
                    need(act, "v_ssq", n - 1)
                    A(sqq, pj, ACT.Square).then_inc(S["a_sqq"], 1)
                if live(n - 1):
                    need(act, "t_tk", n - 1)
                    need(act, "g_kcar", n - 1)
                    A(KT3[:, :, W:], tp.rearrange("p (a t) -> p a t", a=PR), ACT.Copy).then_inc(S["a_KT"], 1)
                if live(n):
                    need(act, "t_pk", n)
                    need(act, "v_ssk", n - 1)
                    A(sqk, pj, ACT.Square).then_inc(S["a_sqk"], 1)
                if live(n - 2):
                    need(act, "t_pT", n - 2)
                    need(act, "t_y1", n - 3)
                    A(pT, tp, ACT.Copy).then_inc(S["a_pT"], 1)

                def exps(a, b):
                    if not live(n - 1):
                        return
                    if a == 0:
                        need(act, "v_nb", n - 1)
                        need(act, "v_ri", n - 2)
                        need(act, "g_pn", n - 2)
                        need(act, "t_pT", n - 2)
                    for h in range(a, b):
                        last = A(pr[:, NK * h:NK * h + NK],
                                 sm[:, NK * h:NK * h + NK], ACT.Exp, scale=q8[1 - u][:, h:h + 1],
                                 bias=nbias[:, h:h + 1], accum_out=rsum[:, h:h + 1])
                    if b == H:
                        last.then_inc(S["a_ex"], 1)

                exps(0, 6)
                if live(n - 2):
                    need(act, "t_y0", n - 2)
                    need(act, "t_o", n - 3)
                    A(heads_first(ysb[0]), by_window(sy), ACT.Copy).then_inc(S["a_y0"], 1)
                exps(6, 11)
                if live(n - 2):
                    need(act, "t_y1", n - 2)
                    A(heads_first(ysb[1]), by_window(tp), ACT.Copy).then_inc(S["a_y1"], 1)
                exps(11, 16)
                if live(n - 4):
                    need(act, "v_gate", n - 4)
                    need(act, "v_h", n - 5)
                    A(gel, gate, ACT.Gelu).then_inc(S["a_gel"], 1)

            run(act, step)
            for i in range(4):
                act.wait_ge(t_fin, i + 1)
                A(arena[:, 2048 + 512 * i:2560 + 512 * i], ps[:, 512 * i:512 * i + 512], ACT.Copy).then_inc(a_fin, 1)

        @block.vector
        def _(dve):
            V = nc.vector
            chained = [0]

            def rsqrt(k, x_, y_, done):
                a_, b_ = nw_a[:, 0:k], nw_b[:, 0:k]
                yield V.tensor_scalar(a_.bitcast(I32), x_.bitcast(I32), 1, None, ALU.logical_shift_right)
                yield V.tensor_scalar(nw_y[:, 0:k].bitcast(I32), a_.bitcast(I32), -1.0, float(MAGIC),
                                      ALU.mult, ALU.add)
                src = nw_y[:, 0:k]
                for i in range(3):
                    yield V.tensor_tensor(a_, x_, src, ALU.mult)
                    yield V.scalar_tensor_tensor(out=b_, in0=a_, scalar=-0.5, in1=src, op0=ALU.mult, op1=ALU.mult)
                    dst = y_ if i == 2 else nw_y[:, 0:k]
                    r = V.scalar_tensor_tensor(out=dst, in0=b_, scalar=1.5, in1=src, op0=ALU.add, op1=ALU.mult)
                    if i < 2:
                        yield r
                    else:
                        done(r)

            def link(ins):
                chained[0] += 1
                ins.then_inc(v_ch, 1)
                dve.wait_ge(v_ch, chained[0])

            dve.wait_ge(a_sig, 1)
            link(V.tensor_scalar(sig, sig, 1.0, None, ALU.add))
            link(V.reciprocal(silu, sig))
            V.tensor_tensor(silu, silu, ccol, ALU.mult).then_inc(v_silu, 1)
            link(V.memset(ones, 1.0))
            dve.wait_ge(s_x, 16)

            def layer_stats(src):
                for t in range(NT):
                    last = V.bn_stats(bnst[:, 6 * t:6 * t + 6], src(t))
                link(last)
                for t in range(NT):
                    last = V.bn_aggr(bnmv[:, 2 * t:2 * t + 2], bnst[:, 6 * t:6 * t + 6])
                link(last)
                var = bnmv.rearrange("p (t k) -> p t k", k=2)[:, :, 1]
                link(V.tensor_scalar(nw_x[:, 0:NT], var, LN_EPS, None, ALU.add))
                for r in rsqrt(NT, nw_x[:, 0:NT], rs16, link):
                    link(r)

            layer_stats(lambda t: xtok[:, t, :])
            for t in range(NT):
                V.tensor_scalar(xntok[:, t, :], xtok[:, t, :], bnmv[:, 2 * t:2 * t + 1], rs16[:, t:t + 1],
                                ALU.subtract, ALU.mult).then_inc(v_xn, 1)
            dve.wait_ge(t_mod, 1)
            link(V.tensor_copy(modT, b7[:, 0:6]))
            link(V.tensor_scalar(ca1, modT[:, 1:2], 1.0, None, ALU.add))
            link(V.tensor_scalar(cb1, modT[:, 4:5], 1.0, None, ALU.add))
            gates = modT.rearrange("p (k j) -> p k j", j=3)[:, :, 2]
            link(V.scalar_tensor_tensor(out=tmpa, in0=gates, scalar=-1.0, in1=gates, op0=ALU.mult, op1=ALU.max))
            link(V.tensor_scalar(tmpa, tmpa, 0.25, None, ALU.max))
            link(V.tensor_scalar(tmpb, gates, 0.0, 2.0, ALU.is_ge, ALU.mult))
            link(V.scalar_tensor_tensor(out=gaf, in0=tmpb[:, 0:1], scalar=-1.0, in1=tmpa[:, 0:1],
                                        op0=ALU.add, op1=ALU.mult))
            V.scalar_tensor_tensor(out=gbf, in0=tmpb[:, 1:2], scalar=-1.0, in1=tmpa[:, 1:2],
                                   op0=ALU.add, op1=ALU.mult).then_inc(v_mod, 1)
            dve.wait_ge(s_wl, 112)
            for j in range(4):
                dve.wait_ge(t_v, j + 1)
                V.tensor_tensor(vtok[:, 512 * j:512 * j + 512].rearrange("p (t d) -> p t d", t=4),
                                ps[:, 512 * j:512 * j + 512].rearrange("p (t d) -> p t d", t=4),
                                bvr[:, None, :].broadcast_to([P, 4, P]), ALU.add).then_inc(v_v, 1)
            for s in range(NT):
                base = T * (s % 2)
                dve.wait_ge(t_s, s + 1)
                d = ps[:, base + P * s:base + P * s + P]
                link(V.tensor_tensor(d, d, diag[:, :], ALU.add))
                link(V.tensor_reduce(mx[:, s:s + 1], ps[:, base + P * s:base + T], AX.X, ALU.max))
                V.tensor_scalar(negm[:, s:s + 1], mx[:, s:s + 1], -SCALE, None, ALU.mult).then_inc(v_nm, 1)
            V.tensor_reduce(mcol, mx, AX.X, ALU.max).then_inc(v_mrow, 1)
            dve.wait_ge(t_mr, 1)
            V.tensor_reduce(mrow[0:1, 0:1], ps[0:1, 0:P], AX.X, ALU.max).then_inc(v_mrow, 1)
            dve.wait_ge(t_mc, 1)
            V.tensor_scalar(mcol, ps[:, 512:513], -SCALE, None, ALU.mult).then_inc(v_mcol, 1)
            dve.wait_ge(a_gs, 1)
            dve.wait_ge(a_e, NT)
            link(V.tensor_tensor(esum, esum, gs, ALU.mult))
            V.tensor_reduce(zc, esum, AX.X, ALU.add).then_inc(v_z, 1)
            dve.wait_ge(t_z, 1)
            link(V.reciprocal(zr, ps[:, 1024:1025]))
            link(V.tensor_scalar(gs, gs, zr, None, ALU.mult))
            v3 = vtok[:, :].rearrange("p (t d) -> p t d", t=NT)
            V.tensor_tensor(v3, v3, gs[:, :, None].broadcast_to([P, NT, P]), ALU.mult).then_inc(v_vs, 1)
            for j in range(4):
                dve.wait_ge(t_av, j + 1)
                d = x1[:, 512 * j:512 * j + 512]
                V.scalar_tensor_tensor(out=d, in0=ps[:, 512 * j:512 * j + 512], scalar=gaf, in1=d,
                                       op0=ALU.mult, op1=ALU.add).then_inc(v_x1, 1)
            dve.wait_ge(t_x1t, 4)
            layer_stats(lambda t: ps[:, T + P * t:T + P * t + P])
            for t in range(NT):
                V.tensor_scalar(xntok[:, t, :], ps[:, T + P * t:T + P * t + P], bnmv[:, 2 * t:2 * t + 1],
                                rs16[:, t:t + 1], ALU.subtract, ALU.mult).then_inc(v_xn2, 1)

            CH = 14
            start = chained[0]

            def heads(ap):
                return ap.rearrange("p (h w d) -> p h w d", h=H, w=2)

            def rot(ap):
                return heads(ap)[:, :, ::-1, :]

            def table(u, k):
                return tabs[u][:, DH * k:DH * k + DH].rearrange("p (w d) -> p w d", w=2)[:, None, :, :]\
                    .broadcast_to([P, H, 2, DH // 2])

            def step(n, u):
                count = [0]

                def chain(ins):
                    count[0] += 1
                    ins.then_inc(v_ch, 1)
                    dve.wait_ge(v_ch, n * CH + (start + count[0]))

                if live(n - 2):
                    need(dve, "a_ex", n - 2)
                    need(dve, "g_pn", n - 3)
                    V.reciprocal(ri_, rsum).then_inc(S["v_ri"], 1)
                if live(n - 1):
                    need(dve, "t_xw", n - 1)
                    need(dve, "t_y1", n - 3)
                    V.tensor_copy(xw[1 - u], b7).then_inc(S["v_xw"], 1)
                if live(n - 5):
                    need(dve, "v_ha", n - 5)
                    need(dve, "a_gel", n - 5)
                    need(dve, "t_th", n - 6)
                    V.tensor_tensor(hh, ha, gel, ALU.mult).then_inc(S["v_h"], 1)
                if live(n):
                    need(dve, "a_sqq", n)
                    need(dve, "g_tab", n)
                    need(dve, "t_tq", n - 1)
                    V.tensor_tensor(heads(qc), heads(pj), table(u, 0), ALU.mult)
                    V.tensor_tensor(heads(qsn), rot(pj), table(u, 1), ALU.mult).then_inc(S["v_qq"], 1)
                if live(n - 5):
                    need(dve, "t_th", n - 5)
                    need(dve, "t_w2", n - 6)
                    V.tensor_copy(hT_[:, 0:2 * P], b6[:, 0:2 * P])
                    V.tensor_copy(hT_[0:85, 2 * P:3 * P], b6[0:85, 2 * P:3 * P]).then_inc(S["v_hT"], 1)
                if live(n - 3):
                    need(dve, "t_to", n - 3)
                    t3 = tile_of(n - 3)
                    V.tensor_tensor(xb[:, bass.ds(t3 * P + 1, P)], b7[:, 0:P], xa[:, bass.ds(t3 * P + PAD, P)],
                                    ALU.add).then_inc(S["v_xb"], 1)
                if live(n - 5):
                    need(dve, "t_w2", n - 5)
                    need(dve, "t_tf", n - 6)
                    V.tensor_copy(fsb, b6[:, 384:512]).then_inc(S["v_f"], 1)
                if live(n - 4):
                    need(dve, "t_xnt", n - 4)
                    need(dve, "t_ha", n - 5)
                    l4 = layer_of(n - 4)
                    V.tensor_scalar(xnT, b7[:, P:2 * P], lngT[:, bass.ds(l4, 1)], lnbT[:, bass.ds(l4, 1)],
                                    ALU.mult, ALU.add).then_inc(S["v_xnT"], 1)
                if live(n):
                    V.tensor_reduce(nw_x[:, 0:16], sqq.rearrange("p (h d) -> p h d", h=H), AX.X, ALU.add)\
                        .then_inc(S["v_ssq"], 1)
                if live(n - 1):
                    need(dve, "t_sc", n - 1)
                    need(dve, "a_ex", n - 2)
                    V.tensor_tensor(sm.rearrange("p (a r k) -> p r a k", r=2, k=NK),
                                    sy.rearrange("p (r a k) -> p r a k", r=2, k=NK),
                                    maskb[:, bass.ds(tile_of(n - 1) * NK, NK)][:, None, None, :]
                                    .broadcast_to([P, 2, PR, NK]), ALU.add).then_inc(S["v_ms"], 1)
                    need(dve, "v_ms", n - 1)
                    V.tensor_reduce(smax, sm.rearrange("p (h k) -> p h k", h=H), AX.X, ALU.max)\
                        .then_inc(S["v_mx"], 1)
                    need(dve, "v_mx", n - 1)
                    V.scalar_tensor_tensor(out=nbias, in0=smax, scalar=-1.0, in1=q8[1 - u],
                                           op0=ALU.mult, op1=ALU.mult).then_inc(S["v_nb"], 1)
                if live(n - 5):
                    need(dve, "t_tf", n - 5)
                    need(dve, "g_xs", n - 4)
                    t5 = tile_of(n - 5)
                    V.scalar_tensor_tensor(out=xa[:, bass.ds(t5 * P + PAD, P)], in0=b6[:, 0:P],
                                           scalar=b2T[:, bass.ds(layer_of(n - 5), 1)],
                                           in1=xb[:, bass.ds(t5 * P + 1, P)], op0=ALU.add, op1=ALU.add)\
                        .then_inc(S["v_xa"], 1)
                if live(n):
                    need(dve, "a_sqk", n)
                    need(dve, "t_tk", n - 1)
                    V.tensor_tensor(heads(kc), heads(pj), table(u, 2), ALU.mult)
                    V.tensor_tensor(heads(ksn), rot(pj), table(u, 3), ALU.mult).then_inc(S["v_kk"], 1)
                    V.tensor_reduce(nw_x[:, 16:32], sqk.rearrange("p (h d) -> p h d", h=H), AX.X, ALU.add)\
                        .then_inc(S["v_ssk"], 1)
                if live(n - 3):
                    need(dve, "t_x2", n - 3)
                    V.tensor_copy(x2c, b6[:, 0:P])
                    V.bn_stats(st2, b6[:, 0:P]).then_inc(S["v_bn"], 1)
                if live(n - 4):
                    need(dve, "t_hg", n - 4)
                    need(dve, "a_gel", n - 5)
                    dve.wait_ge(s_b1, (layer_of(n - 4) + 1) * 16)
                    V.tensor_tensor(gate, b6[:, 0:FI], b1b[:, bass.ds(slot_of(n - 4) * 2 * FI + FI, FI)],
                                    ALU.add).then_inc(S["v_gate"], 1)
                if live(n) or live(n - 3):
                    if live(n - 3):
                        apart(dve)
                        need(dve, "v_bn", n - 3)
                        chain(V.bn_aggr(mv2, st2))
                        chain(V.tensor_scalar(nw_x[:, 32:33], mv2[:, 1:2], LN_EPS, None, ALU.add))
                    else:
                        chain(V.memset(nw_x[:, 32:33], 1.0))
                        chain(V.memset(mv2, 0.0))
                    if live(n):
                        need(dve, "v_ssk", n)
                        need(dve, "v_ssq", n)
                        chain(V.tensor_scalar(nw_x[:, 0:32], nw_x[:, 0:32], NORM_EPS2, None, ALU.max))
                    else:
                        chain(V.memset(nw_x[:, 0:32], 1.0))
                    need(dve, "g_krn", n - 2)
                    for r in rsqrt(33, nw_x[:, 0:33], rk[u], chain):
                        chain(r)
                    assert count[0] == CH
                if live(n):
                    need(dve, "a_ex", n - 2)
                    V.tensor_scalar(q8[u], rk[u][:, 0:16], 8.0, None, ALU.mult).then_inc(S["v_rs"], 1)
                if live(n - 3):
                    need(dve, "t_xnt", n - 4)
                    V.tensor_scalar(xn2, x2c, mv2[:, 0:1], rk[u][:, 32:33], ALU.subtract, ALU.mult)\
                        .then_inc(S["v_lnx"], 1)
                if live(n - 4):
                    need(dve, "t_ha", n - 4)
                    V.tensor_tensor(ha, b6[:, 0:FI], b1b[:, bass.ds(slot_of(n - 4) * 2 * FI, FI)],
                                    ALU.add).then_inc(S["v_ha"], 1)
                if live(n - 2):
                    need(dve, "t_o", n - 2)
                    need(dve, "t_to", n - 3)
                    V.tensor_copy(osb, b7[:, 0:P]).then_inc(S["v_os"], 1)

            dve.wait_ge(s_lnp, 64)
            dve.wait_ge(s_msk, 16)
            dve.wait_ge(a_xa, 4)
            V.memset(mv2, 0.0).then_inc(S["v_xa"], NT)
            run(dve, step)

            need(dve, "v_xa", E - 1)
            for i in range(4):
                d = x1[:, 512 * i:512 * i + 512]
                V.scalar_tensor_tensor(out=d, in0=xa[:, PAD + 512 * i:PAD + 512 * i + 512], scalar=gbf, in1=d,
                                       op0=ALU.mult, op1=ALU.add).then_inc(v_fin, 1)

        @block.gpsimd
        def _(pool):
            G = nc.gpsimd
            pool.wait_ge(t_av, 4)
            G.memset(xa[:, 0:PAD], 0.0).then_inc(g_init, 1)
            G.memset(xb[:, 0:1], 0.0).then_inc(g_init, 1)
            G.memset(KT, 0.0).then_inc(g_init, 1)

            def shifted_input(e, u):
                apart(pool)
                need(pool, "g_tab", e - 1)
                need(pool, "g_kcar", e - 2)
                need(pool, "v_xa", e - NT)
                need(pool, "g_xd", e - 2)
                need(pool, "t_pk", e - 2)
                o = tile_of(e) * P + (PAD - W)
                G.tensor_copy(xs[u][0:64, :], xa[0:64, bass.ds(o, P + W)])
                G.tensor_copy(xs[u][64:128, :], xa[64:128, bass.ds(o - 1, P + W)]).then_inc(S["g_xs"], 1)
                need(pool, "g_xs", e)

            def window_pairs(e, u):
                apart(pool)
                need(pool, "g_xs", e)
                need(pool, "t_xw", e - 1)
                v = xs[u]
                keys = bass.AP(v.tensor, v.offset, [v.ap[0], (W, NW), (0, 2), (1, NK)])
                G.tensor_copy(xd.rearrange("p (j r k) -> p j r k", j=NW, r=2), keys).then_inc(S["g_xd"], 1)

            def scaled_tables(e, u):
                need(pool, "v_kk", e - 2)
                pool.wait_ge(s_scl, (layer_of(e) + 1) * 96)
                G.tensor_tensor(tabs[u], tabb[:, bass.ds(tile_of(e) * 4 * DH, 4 * DH)],
                                scl[:, bass.ds(slot_of(e) * 4 * DH, 4 * DH)], ALU.mult).then_inc(S["g_tab"], 1)

            def step(n, u):
                if live(n - 1):
                    need(pool, "t_sc", n - 2)
                    need(pool, "a_KT", n - 2)
                    G.tensor_tensor(KT3[:, :, 0:W], KT3[:, :, P:P + W],
                                    carry[:, :, None].broadcast_to([P, PR, W]), ALU.mult)\
                        .then_inc(S["g_kcar"], 1)
                if live(n + 1):
                    shifted_input(n + 1, 1 - u)
                    scaled_tables(n + 1, 1 - u)
                if live(n):
                    window_pairs(n, u)
                if live(n - 2):
                    need(pool, "a_ex", n - 2)
                    need(pool, "v_ri", n - 2)
                    p3 = pr.rearrange("p (h k) -> p h k", h=H)
                    G.tensor_tensor(p3, p3, ri_[:, :, None].broadcast_to([P, H, NK]), ALU.mult)\
                        .then_inc(S["g_pn"], 1)
                if live(n - 3):
                    apart(pool)
                    need(pool, "g_pn", n - 2)
                    need(pool, "v_xb", n - 3)
                    need(pool, "t_x2", n - 4)
                    t3 = tile_of(n - 3)
                    G.tensor_copy(xs2[0:64, :], xb[0:64, bass.ds(t3 * P + 1, P)])
                    G.tensor_copy(xs2[64:128, :], xb[64:128, bass.ds(t3 * P, P)]).then_inc(S["g_xs2"], 1)
                    need(pool, "g_xs2", n - 3)
                if live(n):
                    need(pool, "v_qq", n)
                    G.tensor_tensor(qc, qc, qsn, ALU.add).then_inc(S["g_qr"], 1)
                    need(pool, "v_kk", n)
                    G.tensor_tensor(kc, kc, ksn, ALU.add).then_inc(S["g_kr"], 1)
                    need(pool, "v_rs", n)
                    need(pool, "g_kr", n)
                    k3 = kc.rearrange("p (h d) -> p h d", h=H)
                    G.tensor_tensor(k3, k3, rk[u][:, 16:32][:, :, None].broadcast_to([P, H, DH]), ALU.mult)\
                        .then_inc(S["g_krn"], 1)

            pool.wait_ge(a_xa, 4)
            pool.wait_ge(s_tab, 16)
            pool.wait_ge(s_lnp, 64)
            pool.wait_ge(g_init, 3)
            shifted_input(0, 0)
            scaled_tables(0, 0)
            run(pool, step, E - UNROLL)


_INS = ["L0_attn_x", "L0_attn_Wq", "L0_attn_bq", "L0_attn_Wk", "L0_attn_bk", "L0_attn_Wv", "L0_attn_bv",
        "L0_ffn_Wqkv", "L0_ffn_q_scale", "L0_ffn_k_scale", "L0_ffn_Wo", "L0_ffn_ln_g", "L0_ffn_ln_b",
        "L0_ffn_W1", "L0_ffn_b1", "L0_ffn_W2", "L0_ffn_b2", "L0_c", "L0_wmod"]


def kernel(**inputs):
    import concourse.bacc as bacc
    from concourse.bass_utils import run_bass_kernel_spmd

    nc = bacc.Bacc("TRN2", target_bir_lowering=False, num_devices=1)
    by_channel = ("L0_ffn_ln_g", "L0_ffn_ln_b", "L0_ffn_b2", "L0_c")
    arrays = {"in_" + n: np.ascontiguousarray(inputs[n].T if n in by_channel else inputs[n]) for n in _INS}
    for n, a in zip(("eye", "rotary", "mask", "diagonal", "carry"), shape_tables()):
        arrays["const_" + n] = a
    aps = [nc.dram_tensor(n, a.shape, mybir.dt.from_np(a.dtype), kind="ExternalInput").ap()
           for n, a in arrays.items()]
    out = nc.dram_tensor("out", (1, T, P), F32, kind="ExternalOutput").ap()
    program(nc, *aps, out)
    r = run_bass_kernel_spmd(nc, [arrays], core_ids=[0])
    return r.results[0]["out"]
```

```python
from contextlib import ExitStack

import numpy as np

import concourse.bass as bass
from concourse import mybir

F32 = mybir.dt.float32
I32 = mybir.dt.int32
ALU = mybir.AluOpType
ACT = mybir.ActivationFunctionType
AX = mybir.AxisListType

P = 128
T = 2048
NT = T // P
L = 6
H = 16
DH = 64
W = 32
NW = P // W
PR = H // 2
NK = 2 * W
FI = 341
FCH = [(0, 128), (128, 128), (256, 85)]
E = L * NT
BANK = 512
BIG = 1.0e30
MAGIC = 0x5F3759DF
LN_EPS = 1e-5
NORM_EPS2 = 1e-24
FILL, UNROLL = 6, 2
LAST = E + 5
SPLIT = 10


def shape_tables():
    f = np.float32
    half = np.arange(0, DH, 2, dtype=f)
    inv = (f(1.0) / np.power(f(10000.0), half / f(DH))).astype(f)
    t = np.arange(T, dtype=f)
    fr = (t[:, None] * inv[None, :]).astype(f)
    fr = np.concatenate([fr, fr], -1)
    base = (half.astype(np.float64) + 0.4 * DH) / (1.4 * DH)
    sc = base[None, :] ** ((np.arange(T) % P - P // 2) / (W // 2))[:, None]
    sc = np.concatenate([sc, sc], -1)
    carry = np.tile(base ** (P / (W // 2)), P // len(base))[:, None]
    cos, sin = np.cos(fr).astype(f), np.sin(fr).astype(f)
    sgn = np.concatenate([-np.ones(DH // 2, f), np.ones(DH // 2, f)])
    iv = 1.0 / sc
    tab = np.stack([cos * sc, sin * sgn * sc, cos * iv, sin * sgn * iv], 1).astype(f)
    tab = tab.reshape(NT, P, 4 * DH).transpose(1, 0, 2).reshape(P, NT * 4 * DH)
    q = np.arange(P)
    i, j = (q % W)[:, None], np.arange(NK)[None, :]
    m = np.where((j >= i) & (j <= i + W), 0.0, -BIG)
    mask = np.repeat(m[:, None, :], NT, 1)
    mask[:W, 0, :W] = -BIG
    diag = np.where(q[None, :] >= q[:, None], 0.0, -BIG)
    return [np.ascontiguousarray(a, f) for a in (np.eye(P), tab, mask.reshape(P, NT * NK), diag, carry)]


def program(nc, x, wq, bq, wk, bk, wv, bv, wqkv, qs, ks, wo, lng, lnb, w1, b1, w2, b2, c, wmod,
            eye, tab, maskt, diagt, carryt, out):
    SCALE = float(P) ** -0.5
    ctx = ExitStack()
    with ctx:
        def sb(name, *shape, dt=F32):
            return ctx.enter_context(nc.sbuf_tensor(name, [P, *shape], dt))

        def sem(name):
            return ctx.enter_context(nc.semaphore(name))

        ident = sb("ident", P)
        diag = sb("diag", P)
        maskb = sb("maskb", NT * NK)
        tabb = sb("tabb", NT * 4 * DH)
        wqk = sb("wqk", 2 * 2048)
        w1b = sb("w1b", 2 * 2 * FI)
        b1b = sb("b1b", 2 * 2 * FI)
        w2b = sb("w2b", 2 * 3 * P)
        scl = sb("scl", 2 * 4 * DH)
        wvo = sb("wvo", L * H * P)
        PAD = W + 1
        xa = sb("xa", PAD + T)
        xb = sb("xb", 1 + T)
        x1 = sb("x1", T)
        vtok = sb("vtok", T)
        arena = sb("arena", 136 * P)
        small = sb("small", 1024)
        at = [0]

        def cols(n):
            at[0] += n
            return small[:, at[0] - n:at[0]]

        ccol, sig, silu = cols(1), cols(1), cols(1)
        modT, ca1, cb1, gaf, gbf, tmpa, tmpb = cols(6), cols(1), cols(1), cols(1), cols(1), cols(2), cols(2)
        bqc, bkc = cols(1), cols(1)
        bvr = cols(P)
        bnst, bnmv, rs16 = cols(6 * NT), cols(2 * NT), cols(NT)
        mx, negm, esum, gs, zc, zr, mcol = cols(NT), cols(NT), cols(NT), cols(NT), cols(1), cols(1), cols(1)
        mrow, ones = cols(P), cols(P)
        lngT, lnbT, b2T = cols(L), cols(L), cols(L)
        nw_x, nw_y, nw_a, nw_b = cols(33), cols(33), cols(33), cols(33)
        ri_, carry = cols(16), cols(1)
        st2, mv2 = cols(6), cols(2)
        rk = [cols(33), cols(33)]
        q8 = [cols(16), cols(16)]
        smax, nbias, rsum, dummy = cols(16), [cols(16), cols(16)], cols(16), cols(1)

        wmod_s = arena[:, 0:768]
        wq_s, wk_s, wv_s = arena[:, 768:896], arena[:, 896:1024], arena[:, 1024:1152]
        xtok = arena[:, 2048:4096].rearrange("p (t d) -> p t d", t=NT)
        xntok = arena[:, 4096:6144].rearrange("p (t d) -> p t d", t=NT)
        wv_st = [arena[:, 6144 + 1024 * i:7168 + 1024 * i] for i in range(2)]
        wo_st = [arena[:, 8192 + 1024 * i:9216 + 1024 * i] for i in range(2)]
        wvT = arena[:, 10240:11264]
        hT, qT0, kT0 = xa[:, 0:T], xb[:, 0:T], wqk[:, 2048:4096]
        eoff = [0]
        for s in range(NT):
            eoff.append(eoff[-1] + T - P * s)

        off = [0]

        def buf(n):
            off[0] += n
            return arena[:, off[0] - n:off[0]]

        xs = [buf(P + W), buf(P + W)]
        xd = buf(NW * 2 * NK)
        xw = [buf(NW * P), buf(NW * P)]
        tabs = [buf(4 * DH), buf(4 * DH)]
        sqq, sqk = buf(1024), buf(1024)
        qc, qsn, kc, ksn = buf(1024), buf(1024), buf(1024), buf(1024)
        QT, KT = buf(1024), buf(PR * (P + W))
        sm, pr, pT = buf(1024), buf(1024), buf(1024)
        ysb = [buf(1024), buf(1024)]
        osb, xs2, xn2, xnT, x2c = buf(P), buf(P), buf(P), buf(P), buf(P)
        gate, gel, ha, hh = (vtok[:, FI * i:FI * i + FI] for i in range(4))
        hT_, fsb = vtok[:, 4 * FI:4 * FI + 3 * P], vtok[:, 4 * FI + 3 * P:4 * FI + 4 * P]
        QT3 = QT.rearrange("p (a t) -> p a t", a=PR)
        KT3 = KT.rearrange("p (a t) -> p a t", a=PR)
        pT3 = pT.rearrange("p (a t) -> p a t", a=PR)

        ps = ctx.enter_context(nc.psum_tensor("ps", [P, 8 * BANK], F32))
        pj = ps[:, 0:1024]
        tp = ps[:, 1024:2048]
        sy = ps[:, 2048:3072]
        b6 = ps[:, 3072:3584]
        b7 = ps[:, 3584:4096]

        s_x, s_cw, s_wl, s_small = sem("s_x"), sem("s_cw"), sem("s_wl"), sem("s_small")
        s_id, s_wqk, s_w1, s_b1, s_w2 = sem("s_id"), sem("s_wqk"), sem("s_w1"), sem("s_b1"), sem("s_w2")
        s_scl, s_tab, s_msk, s_lnp = sem("s_scl"), sem("s_tab"), sem("s_msk"), sem("s_lnp")
        s_wst = [sem("s_wst0"), sem("s_wst1")]
        s_out = sem("s_out")
        v_ch = sem("v_ch")
        a_sig, v_silu, t_mod, v_mod = sem("a_sig"), sem("v_silu"), sem("t_mod"), sem("v_mod")
        v_xn, t_xT, t_xnT, a_x1, a_hT = sem("v_xn"), sem("t_xT"), sem("t_xnT"), sem("a_x1"), sem("a_hT")
        t_q, t_k, t_v, a_qk, v_v = sem("t_q"), sem("t_k"), sem("t_v"), sem("a_qk"), sem("v_v")
        t_wvT, a_wvT, t_m, a_m = sem("t_wvT"), sem("a_wvT"), sem("t_m"), sem("a_m")
        t_s, v_nm, a_e = sem("t_s"), sem("v_nm"), sem("a_e")
        t_mr, v_mrow, t_mc, v_mcol, a_gs, v_z, t_z, v_vs = (sem("t_mr"), sem("v_mrow"), sem("t_mc"), sem("v_mcol"),
                                                    sem("a_gs"), sem("v_z"), sem("t_z"), sem("v_vs"))
        t_av, v_x1, t_x1t, v_xn2, t_x2T, a_xa = (sem("t_av"), sem("v_x1"), sem("t_x1t"), sem("v_xn2"),
                                                 sem("t_x2T"), sem("a_xa"))
        g_init = sem("g_init")
        v_fin, t_fin, a_fin = sem("v_fin"), sem("t_fin"), sem("a_fin")
        names = ("g_h g_xs g_xd g_tab g_qr g_kr g_krn g_pn g_xs2 g_kcar "
                 "t_tq t_tk t_xw t_pq t_pk t_sc t_pT t_y0 t_y1 t_o t_to t_x2 t_xnt t_hg t_ha t_th t_w2 t_tf "
                 "a_sqq a_sqk a_QT a_KT a_ex a_pT a_y0 a_y1 a_gel "
                 "v_xw v_f v_xb v_qq v_xa v_xnT v_ssq v_ms v_nb v_bn v_kk v_ssk v_gate v_ha v_rs v_mx v_lnx v_os v_hT v_ri")
        S = {n: sem("p" + n) for n in names.split()}

        block = ctx.enter_context(nc.Block())

        def need(eng, name, e):
            if isinstance(e, int):
                e = min(e, E - 1)
                if e + ahead.get(name, 0) < 0:
                    return
            eng.wait_ge(S[name], e + (ahead.get(name, 0) + 1))

        ahead = {"v_xa": NT}

        def apart(eng):
            eng.wait_ge(s_id, 16)

        def live(e):
            return not isinstance(e, int) or 0 <= e < E

        def run(eng, step, end=E):
            for n in range(FILL):
                step(n, n % 2)
            with eng.Fori(FILL, end, UNROLL) as i:
                for u in range(UNROLL):
                    step(i + u, u)
            for n in range(end, LAST):
                step(n, n % 2)

        def tile_of(e):
            return e % NT

        def layer_of(e):
            return e // NT

        def slot_of(e):
            return (e // NT) % 2

        @block.sync
        def _(sp):
            sp.dma_start(xtok, x[0].rearrange("(t p) d -> p t d", p=P)).then_inc(s_x, 16)
            sp.dma_start(ident[:, :], eye).then_inc(s_id, 16)
            sp.dma_start(ccol, c).then_inc(s_cw, 16)
            sp.dma_start(wmod_s, wmod).then_inc(s_cw, 16)
            sp.dma_start(wq_s, wq).then_inc(s_wl, 16)
            sp.dma_start(wk_s, wk).then_inc(s_wl, 16)
            sp.dma_start(wv_s, wv).then_inc(s_wl, 16)
            sp.dma_start(bqc, bq.rearrange("(d a) -> d a", a=1)).then_inc(s_wl, 16)
            sp.dma_start(bkc, bk.rearrange("(d a) -> d a", a=1)).then_inc(s_wl, 16)
            sp.dma_start(bvr, bv.partition_broadcast(P)).then_inc(s_wl, 16)
            sp.dma_start(diag[:, :], diagt).then_inc(s_wl, 16)
            for l in range(L):
                if l >= 2:
                    sp.wait_ge(t_m, l - 1)
                sp.dma_start(wv_st[l % 2], wqkv[l, :, 2048:3072]).then_inc(s_wst[l % 2], 16)
                sp.dma_start(wo_st[l % 2].rearrange("p (a d) -> p a d", a=PR),
                             wo[l].rearrange("(a p) d -> p a d", p=P)).then_inc(s_wst[l % 2], 16)
            sp.dma_start(maskb[:, :], maskt).then_inc(s_msk, 16)
            sp.dma_start(tabb[:, :], tab).then_inc(s_tab, 16)
            sp.dma_start(carry, carryt).then_inc(s_lnp, 16)
            sp.dma_start(lngT, lng).then_inc(s_lnp, 16)
            sp.dma_start(lnbT, lnb).then_inc(s_lnp, 16)
            sp.dma_start(b2T, b2).then_inc(s_lnp, 16)

            def layer_weights(l):
                o = (l % 2)
                def dst(t, n):
                    return t[:, bass.ds(o * n, n)]
                sp.dma_start(dst(wqk, 2048), wqkv[l, :, 0:2048]).then_inc(s_wqk, 16)
                sp.dma_start(dst(w1b, 2 * FI), w1[l]).then_inc(s_w1, 16)
                sp.dma_start(dst(b1b, 2 * FI), b1[l].partition_broadcast(P)).then_inc(s_b1, 16)
                w2d = dst(w2b, 3 * P)
                for j, (k0, kn) in enumerate(FCH):
                    sp.dma_start(w2d[0:kn, j * P:(j + 1) * P], w2[l, k0:k0 + kn, :]).then_inc(s_w2, 16)
                for j, (r, lo) in enumerate(((qs, 0), (qs, 1), (ks, 0), (ks, 1))):
                    sd = dst(scl, 4 * DH)
                    if lo == 0:
                        sp.dma_start(sd[:, j * DH:(j + 1) * DH], r[l].partition_broadcast(P)).then_inc(s_scl, 16)
                    else:
                        for a in range(2):
                            sp.dma_start(sd[:, j * DH + 32 * a:j * DH + 32 * a + 32],
                                         r[l, 32 - 32 * a:64 - 32 * a].partition_broadcast(P)).then_inc(s_scl, 16)

            layer_weights(0)
            sp.wait_ge(t_s, NT)
            for s_, v_ in ((s_wqk, 16), (s_w1, 16), (s_b1, 16), (s_w2, 48), (s_scl, 96)):
                sp.wait_ge(s_, v_)
            layer_weights(1)
            with sp.Fori(2, L) as l:
                through = sp.snap(l * NT - (NT - 1))
                apart(sp)
                sp.wait_ge(S["t_w2"], through)
                layer_weights(l)
            for i in range(4):
                sp.wait_ge(a_fin, i + 1)
                sp.dma_start(out[0, 512 * i:512 * i + 512].rearrange("(t p) d -> p t d", p=P),
                             xtok[:, 4 * i:4 * i + 4, :]).then_inc(s_out, 16)
            sp.wait_ge(s_out, 64)

        @block.tensor
        def _(pe):
            mm = nc.tensor.matmul

            def tr(o, i, n=P):
                return nc.tensor.transpose(o, i, ident[0:n, 0:n])

            pe.wait_ge(s_cw, 32)
            pe.wait_ge(v_silu, 1)
            for j in range(6):
                last = mm(b7[:, j:j + 1], wmod_s[:, j * P:(j + 1) * P], silu, start=True, stop=True)
            last.then_inc(t_mod, 1)
            pe.wait_ge(s_x, 16)
            pe.wait_ge(s_id, 16)
            for t in range(NT):
                last = tr(ps[:, P * t:P * t + P], xtok[:, t, :])
                if t % 4 == 3:
                    last.then_inc(t_xT, 1)
            pe.wait_ge(v_mod, 1)
            for t in range(NT):
                if t % 4 == 0:
                    pe.wait_ge(v_xn, t + 4)
                last = tr(ps[:, T + P * t:T + P * t + P], xntok[:, t, :])
                if t % 4 == 3:
                    last.then_inc(t_xnT, 1)
            pe.wait_ge(s_wl, 112)
            for j in range(4):
                pe.wait_ge(a_x1, j + 1)
                pe.wait_ge(a_hT, j + 1)
                mm(ps[:, 512 * j:512 * j + 512], wq_s, hT[:, 512 * j:512 * j + 512],
                   start=True, stop=True).then_inc(t_q, 1)
            for j in range(4):
                mm(ps[:, T + 512 * j:T + 512 * j + 512], wk_s, hT[:, 512 * j:512 * j + 512],
                   start=True, stop=True).then_inc(t_k, 1)
            for t in range(NT):
                if t % 4 == 0:
                    pe.wait_ge(a_qk, t // 4 + 1)
                last = mm(ps[:, P * t:P * t + P], hT[:, P * t:P * t + P], wv_s, start=True, stop=True)
                if t % 4 == 3:
                    last.then_inc(t_v, 1)
            for l in range(L):
                pe.wait_ge(s_wst[l % 2], 32 * (l // 2 + 1))
                if l == 0:
                    pe.wait_ge(v_v, 2)
                    pe.wait_ge(a_qk, 8)
                else:
                    pe.wait_ge(a_wvT, l)
                for p in range(PR):
                    last = tr(ps[:, P * p:P * p + P], wv_st[l % 2][:, P * p:P * p + P])
                last.then_inc(t_wvT, 1)
                pe.wait_ge(a_wvT, l + 1)
                if l:
                    pe.wait_ge(a_m, l)
                for p in range(PR):
                    for r in range(2):
                        last = mm(ps[:, T + 1024 * r + P * p:T + 1024 * r + P * p + P],
                                  wvT[DH * r:DH * r + DH, P * p:P * p + P],
                                  wo_st[l % 2][DH * r:DH * r + DH, P * p:P * p + P], start=True, stop=True)
                last.then_inc(t_m, 1)
            pe.wait_ge(v_v, 4)
            pe.wait_ge(a_m, L)
            for s in range(NT):
                base = T * (s % 2)
                if s >= 2:
                    pe.wait_ge(a_e, s - 1)
                for j in range(s // 4, 4):
                    lo = max(512 * j, P * s)
                    last = mm(ps[:, base + lo:base + 512 * j + 512], kT0[:, P * s:P * s + P],
                              qT0[:, lo:512 * j + 512], start=True, stop=True)
                last.then_inc(t_s, 1)
            pe.wait_ge(v_mrow, 1)
            tr(ps[0:1, 0:P], mcol).then_inc(t_mr, 1)
            pe.wait_ge(v_mrow, 2)
            mm(ps[:, 512:513], ones[0:1, :], mrow[0:1, 0:1], start=True, stop=True).then_inc(t_mc, 1)
            pe.wait_ge(v_z, 1)
            mm(ps[:, 1024:1025], ones, zc, start=True, stop=True).then_inc(t_z, 1)
            pe.wait_ge(v_vs, 1)
            for j in range(4):
                for s in range(4 * j + 4):
                    lo = max(512 * j, P * s)
                    last = mm(ps[:, lo:512 * j + 512], vtok[:, P * s:P * s + P],
                              arena[:, eoff[s] + lo - P * s:eoff[s] + 512 * j + 512 - P * s],
                              start=(s == 0), stop=(s == 4 * j + 3))
                last.then_inc(t_av, 1)
            for j in range(4):
                pe.wait_ge(v_x1, j + 1)
                for t in range(4 * j, 4 * j + 4):
                    last = tr(ps[:, T + P * t:T + P * t + P], x1[:, P * t:P * t + P])
                last.then_inc(t_x1t, 1)
            for j in range(4):
                pe.wait_ge(v_xn2, 4 * j + 4)
                for t in range(4 * j, 4 * j + 4):
                    last = tr(ps[:, P * t:P * t + P], xntok[:, t, :])
                last.then_inc(t_x2T, 1)

            def project(n, u, part, j):
                return mm(pj[:, 512 * j:512 * j + 512], xs[u][:, W:],
                          wqk[:, bass.ds(slot_of(n) * 2048 + (1024 * part + 512 * j), 512)],
                          start=True, stop=True)

            def scores(pairs):
                for p in pairs:
                    for r in range(2):
                        for j in range(NW):
                            last = mm(sy[W * j:W * j + W, 512 * r + NK * p:512 * r + NK * p + NK],
                                      QT3[DH * r:DH * r + DH, p, W * j:W * j + W],
                                      KT3[DH * r:DH * r + DH, p, W * j:W * j + NK], start=True, stop=True)
                return last

            def values(u, r, o):
                for j in range(NW):
                    last = mm(o[:, 256 * j:256 * j + 256].rearrange("p (a q) -> p a q", a=PR),
                              xw[u][DH * r:DH * r + DH, P * j:P * j + P],
                              pT3[DH * r:DH * r + DH, :, W * j:W * j + W], start=True, stop=True)
                return last

            def output(e, r):
                for p in range(PR):
                    last = mm(b7[:, 0:P], ysb[r][:, P * p:P * p + P],
                              wvo[:, bass.ds(layer_of(e) * (H * P) + (r * PR + p) * P, P)],
                              start=(r == 1 and p == 0), stop=(r == 0 and p == PR - 1))
                return last

            def step(n, u):
                if live(n):
                    need(pe, "g_xs", n)
                    need(pe, "a_sqk", n - 1)
                    need(pe, "v_kk", n - 1)
                    pe.wait_ge(s_wqk, (layer_of(n) + 1) * 16)
                    project(n, u, 0, 0)
                    project(n, u, 0, 1).then_inc(S["t_pq"], 1)
                if live(n - 3):
                    need(pe, "a_y0", n - 3)
                    output(n - 3, 0).then_inc(S["t_o"], 1)
                if live(n - 1):
                    need(pe, "g_krn", n - 1)
                    need(pe, "a_QT", n - 1)
                    for p in range(PR):
                        last = tr(tp[:, P * p:P * p + P], kc[:, P * p:P * p + P])
                    last.then_inc(S["t_tk"], 1)
                if live(n - 5):
                    need(pe, "v_hT", n - 5)
                    pe.wait_ge(s_w2, (layer_of(n - 5) + 1) * 48)
                    for j, (k0, kn) in enumerate(FCH):
                        last = mm(b6[:, 384:512], hT_[0:kn, P * j:P * j + P],
                                  w2b[0:kn, bass.ds(slot_of(n - 5) * 3 * P + P * j, P)],
                                  start=(j == 0), stop=(j == 2))
                    last.then_inc(S["t_w2"], 1)
                if live(n - 1):
                    need(pe, "g_xd", n - 1)
                    need(pe, "v_os", n - 3)
                    for j in range(NW):
                        last = tr(b7[:, P * j:P * j + P], xd[:, P * j:P * j + P])
                    last.then_inc(S["t_xw"], 1)
                if live(n - 1):
                    apart(pe)
                    need(pe, "a_KT", n - 1)
                    need(pe, "g_kcar", n - 1)
                    scores(range(0, 1))
                if live(n - 5):
                    need(pe, "v_f", n - 5)
                    tr(b6[:, 0:P], fsb).then_inc(S["t_tf"], 1)
                if live(n - 1):
                    scores(range(1, 3))
                if live(n - 3):
                    need(pe, "v_os", n - 3)
                    need(pe, "v_xw", n - 1)
                    tr(b7[:, 0:P], osb).then_inc(S["t_to"], 1)
                if live(n - 1):
                    scores(range(3, 4))
                if live(n):
                    need(pe, "a_sqq", n)
                    need(pe, "v_qq", n)
                    project(n, u, 1, 0)
                    project(n, u, 1, 1).then_inc(S["t_pk"], 1)
                if live(n - 4):
                    need(pe, "v_lnx", n - 4)
                    need(pe, "v_xb", n - 3)
                    tr(b7[:, P:2 * P], xn2).then_inc(S["t_xnt"], 1)
                if live(n - 1):
                    scores(range(4, 6))
                if live(n - 4):
                    need(pe, "v_xnT", n - 4)
                    need(pe, "v_xa", n - 5)
                    pe.wait_ge(s_w1, (layer_of(n - 4) + 1) * 16)
                    mm(b6[:, 0:FI], xnT, w1b[:, bass.ds(slot_of(n - 4) * 2 * FI + FI, FI)],
                       start=True, stop=True).then_inc(S["t_hg"], 1)
                if live(n - 2):
                    need(pe, "g_pn", n - 2)
                    need(pe, "a_KT", n - 1)
                    for p in range(PR):
                        last = tr(tp[:, P * p:P * p + P], pr[:, P * p:P * p + P])
                    last.then_inc(S["t_pT"], 1)
                if live(n - 1):
                    scores(range(6, 7))
                if live(n - 4):
                    need(pe, "v_gate", n - 4)
                    mm(b6[:, 0:FI], xnT, w1b[:, bass.ds(slot_of(n - 4) * 2 * FI, FI)],
                       start=True, stop=True).then_inc(S["t_ha"], 1)
                if live(n - 1):
                    scores(range(7, 8)).then_inc(S["t_sc"], 1)
                if live(n - 2):
                    need(pe, "a_pT", n - 2)
                    need(pe, "v_xw", n - 2)
                    values(u, 1, tp).then_inc(S["t_y1"], 1)
                if live(n - 3):
                    need(pe, "g_xs2", n - 3)
                    need(pe, "v_ha", n - 4)
                    tr(b6[:, 0:P], xs2).then_inc(S["t_x2"], 1)
                if live(n - 2):
                    need(pe, "v_ms", n - 1)
                    values(u, 0, sy).then_inc(S["t_y0"], 1)
                if live(n - 4):
                    need(pe, "g_h", n - 4)
                    need(pe, "v_bn", n - 3)
                    for j, (k0, kn) in enumerate(FCH):
                        last = tr(b6[0:kn, P * j:P * j + P], hh[:, k0:k0 + kn])
                    last.then_inc(S["t_th"], 1)
                if live(n):
                    need(pe, "g_qr", n)
                    need(pe, "a_y1", n - 2)
                    for p in range(PR):
                        last = tr(tp[:, P * p:P * p + P], qc[:, P * p:P * p + P])
                    last.then_inc(S["t_tq"], 1)
                if live(n - 2):
                    need(pe, "v_xb", n - 3)
                    need(pe, "v_xnT", n - 4)
                    need(pe, "a_y1", n - 2)
                    output(n - 2, 1)

            pe.wait_ge(a_xa, 4)
            pe.wait_ge(g_init, 3)
            run(pe, step)

            for i in range(4):
                pe.wait_ge(v_fin, i + 1)
                for t in range(4 * i, 4 * i + 4):
                    last = tr(ps[:, P * t:P * t + P], x1[:, P * t:P * t + P])
                last.then_inc(t_fin, 1)

        @block.scalar
        def _(act):
            A = nc.scalar.activation

            def heads_first(ap):
                return ap.rearrange("d (a j q) -> d j a q", j=NW, a=PR)

            def by_window(ap):
                return ap.rearrange("d (j a q) -> d j a q", j=NW, a=PR)

            act.wait_ge(s_cw, 32)
            A(sig, ccol, ACT.Exp, scale=-1.0).then_inc(a_sig, 1)
            for j in range(4):
                act.wait_ge(t_xT, j + 1)
                A(x1[:, 512 * j:512 * j + 512], ps[:, 512 * j:512 * j + 512], ACT.Copy).then_inc(a_x1, 1)
            act.wait_ge(v_mod, 1)
            for j in range(4):
                act.wait_ge(t_xnT, j + 1)
                A(hT[:, 512 * j:512 * j + 512], ps[:, T + 512 * j:T + 512 * j + 512], ACT.Identity,
                  scale=ca1, bias=modT[:, 0:1]).then_inc(a_hT, 1)
            act.wait_ge(s_wl, 112)
            for j in range(4):
                act.wait_ge(t_q, j + 1)
                A(qT0[:, 512 * j:512 * j + 512], ps[:, 512 * j:512 * j + 512], ACT.Identity,
                  bias=bqc).then_inc(a_qk, 1)
            for j in range(4):
                act.wait_ge(t_k, j + 1)
                A(kT0[:, 512 * j:512 * j + 512], ps[:, T + 512 * j:T + 512 * j + 512], ACT.Identity,
                  bias=bkc).then_inc(a_qk, 1)
            for l in range(L):
                act.wait_ge(t_wvT, l + 1)
                if l:
                    act.wait_ge(t_m, l)
                A(wvT, ps[:, 0:1024], ACT.Copy).then_inc(a_wvT, 1)
                act.wait_ge(t_m, l + 1)
                A(wvo[:, l * H * P:(l + 1) * H * P], ps[:, T:T + H * P], ACT.Copy).then_inc(a_m, 1)
            act.wait_ge(v_v, 4)
            for s in range(NT):
                act.wait_ge(v_nm, s + 1)
                base = T * (s % 2)
                A(arena[:, eoff[s]:eoff[s + 1]], ps[:, base + P * s:base + T], ACT.Exp,
                  scale=SCALE, bias=negm[:, s:s + 1], accum_out=esum[:, s:s + 1]).then_inc(a_e, 1)
            act.wait_ge(v_mcol, 1)
            A(gs, mx, ACT.Exp, scale=SCALE, bias=mcol).then_inc(a_gs, 1)
            act.wait_ge(g_init, 3)
            for j in range(4):
                act.wait_ge(t_x2T, j + 1)
                A(xa[:, PAD + 512 * j:PAD + 512 * j + 512], ps[:, 512 * j:512 * j + 512], ACT.Identity,
                  scale=cb1, bias=modT[:, 3:4]).then_inc(a_xa, 1)

            def exps(e, u, a, b):
                for h in range(a, b):
                    last = A(pr[:, NK * h:NK * h + NK], sm[:, NK * h:NK * h + NK], ACT.Exp,
                             scale=q8[u][:, h:h + 1], bias=nbias[u][:, h:h + 1], accum_out=rsum[:, h:h + 1])
                return last

            def step(n, u):
                if live(n):
                    need(act, "t_pq", n)
                    need(act, "v_ssq", n - 1)
                    A(sqq, pj, ACT.Square).then_inc(S["a_sqq"], 1)
                if live(n - 2):
                    exps(n - 2, u, SPLIT, H).then_inc(S["a_ex"], 1)
                if live(n - 1):
                    need(act, "t_tk", n - 1)
                    need(act, "g_kcar", n - 1)
                    A(KT3[:, :, W:], tp.rearrange("p (a t) -> p a t", a=PR), ACT.Copy).then_inc(S["a_KT"], 1)
                if live(n):
                    need(act, "t_pk", n)
                    need(act, "v_ssk", n - 1)
                    A(sqk, pj, ACT.Square).then_inc(S["a_sqk"], 1)
                if live(n - 2):
                    need(act, "t_pT", n - 2)
                    need(act, "t_y0", n - 3)
                    A(pT, tp, ACT.Copy).then_inc(S["a_pT"], 1)
                if live(n - 4):
                    need(act, "v_gate", n - 4)
                    need(act, "g_h", n - 5)
                    A(gel, gate, ACT.Gelu).then_inc(S["a_gel"], 1)
                if live(n - 2):
                    need(act, "t_y1", n - 2)
                    need(act, "t_o", n - 3)
                    A(heads_first(ysb[1]), by_window(tp), ACT.Copy).then_inc(S["a_y1"], 1)
                    A(dummy, ones[:, 0:1], ACT.Exp)
                    need(act, "t_y0", n - 2)
                    A(heads_first(ysb[0]), by_window(sy), ACT.Copy).then_inc(S["a_y0"], 1)
                if live(n):
                    need(act, "t_tq", n)
                    need(act, "t_sc", n - 1)
                    A(QT, tp, ACT.Copy).then_inc(S["a_QT"], 1)
                if live(n - 1):
                    need(act, "v_nb", n - 1)
                    need(act, "v_ri", n - 2)
                    need(act, "t_pT", n - 2)
                    exps(n - 1, 1 - u, 0, SPLIT)

            run(act, step)
            for i in range(4):
                act.wait_ge(t_fin, i + 1)
                A(arena[:, 2048 + 512 * i:2560 + 512 * i], ps[:, 512 * i:512 * i + 512], ACT.Copy).then_inc(a_fin, 1)

        @block.vector
        def _(dve):
            V = nc.vector
            chained = [0]

            def rsqrt(k, x_, y_, done):
                a_, b_ = nw_a[:, 0:k], nw_b[:, 0:k]
                yield V.tensor_scalar(a_.bitcast(I32), x_.bitcast(I32), 1, None, ALU.logical_shift_right)
                yield V.tensor_scalar(nw_y[:, 0:k].bitcast(I32), a_.bitcast(I32), -1.0, float(MAGIC),
                                      ALU.mult, ALU.add)
                src = nw_y[:, 0:k]
                for i in range(3):
                    yield V.tensor_tensor(a_, x_, src, ALU.mult)
                    yield V.scalar_tensor_tensor(out=b_, in0=a_, scalar=-0.5, in1=src, op0=ALU.mult, op1=ALU.mult)
                    dst = y_ if i == 2 else nw_y[:, 0:k]
                    r = V.scalar_tensor_tensor(out=dst, in0=b_, scalar=1.5, in1=src, op0=ALU.add, op1=ALU.mult)
                    if i < 2:
                        yield r
                    else:
                        done(r)

            def link(ins):
                chained[0] += 1
                ins.then_inc(v_ch, 1)
                dve.wait_ge(v_ch, chained[0])

            dve.wait_ge(a_sig, 1)
            link(V.tensor_scalar(sig, sig, 1.0, None, ALU.add))
            link(V.reciprocal(silu, sig))
            V.tensor_tensor(silu, silu, ccol, ALU.mult).then_inc(v_silu, 1)
            link(V.memset(ones, 1.0))
            dve.wait_ge(s_x, 16)

            def layer_stats(src):
                for t in range(NT):
                    last = V.bn_stats(bnst[:, 6 * t:6 * t + 6], src(t))
                link(last)
                for t in range(NT):
                    last = V.bn_aggr(bnmv[:, 2 * t:2 * t + 2], bnst[:, 6 * t:6 * t + 6])
                link(last)
                var = bnmv.rearrange("p (t k) -> p t k", k=2)[:, :, 1]
                link(V.tensor_scalar(nw_x[:, 0:NT], var, LN_EPS, None, ALU.add))
                for r in rsqrt(NT, nw_x[:, 0:NT], rs16, link):
                    link(r)

            layer_stats(lambda t: xtok[:, t, :])
            for t in range(NT):
                V.tensor_scalar(xntok[:, t, :], xtok[:, t, :], bnmv[:, 2 * t:2 * t + 1], rs16[:, t:t + 1],
                                ALU.subtract, ALU.mult).then_inc(v_xn, 1)
            dve.wait_ge(t_mod, 1)
            link(V.tensor_copy(modT, b7[:, 0:6]))
            link(V.tensor_scalar(ca1, modT[:, 1:2], 1.0, None, ALU.add))
            link(V.tensor_scalar(cb1, modT[:, 4:5], 1.0, None, ALU.add))
            gates = modT.rearrange("p (k j) -> p k j", j=3)[:, :, 2]
            link(V.scalar_tensor_tensor(out=tmpa, in0=gates, scalar=-1.0, in1=gates, op0=ALU.mult, op1=ALU.max))
            link(V.tensor_scalar(tmpa, tmpa, 0.25, None, ALU.max))
            link(V.tensor_scalar(tmpb, gates, 0.0, 2.0, ALU.is_ge, ALU.mult))
            link(V.scalar_tensor_tensor(out=gaf, in0=tmpb[:, 0:1], scalar=-1.0, in1=tmpa[:, 0:1],
                                        op0=ALU.add, op1=ALU.mult))
            V.scalar_tensor_tensor(out=gbf, in0=tmpb[:, 1:2], scalar=-1.0, in1=tmpa[:, 1:2],
                                   op0=ALU.add, op1=ALU.mult).then_inc(v_mod, 1)
            dve.wait_ge(s_wl, 112)
            for j in range(4):
                dve.wait_ge(t_v, j + 1)
                V.tensor_tensor(vtok[:, 512 * j:512 * j + 512].rearrange("p (t d) -> p t d", t=4),
                                ps[:, 512 * j:512 * j + 512].rearrange("p (t d) -> p t d", t=4),
                                bvr[:, None, :].broadcast_to([P, 4, P]), ALU.add).then_inc(v_v, 1)
            for s in range(NT):
                base = T * (s % 2)
                dve.wait_ge(t_s, s + 1)
                d = ps[:, base + P * s:base + P * s + P]
                link(V.tensor_tensor(d, d, diag[:, :], ALU.add))
                link(V.tensor_reduce(mx[:, s:s + 1], ps[:, base + P * s:base + T], AX.X, ALU.max))
                V.tensor_scalar(negm[:, s:s + 1], mx[:, s:s + 1], -SCALE, None, ALU.mult).then_inc(v_nm, 1)
            V.tensor_reduce(mcol, mx, AX.X, ALU.max).then_inc(v_mrow, 1)
            dve.wait_ge(t_mr, 1)
            V.tensor_reduce(mrow[0:1, 0:1], ps[0:1, 0:P], AX.X, ALU.max).then_inc(v_mrow, 1)
            dve.wait_ge(t_mc, 1)
            V.tensor_scalar(mcol, ps[:, 512:513], -SCALE, None, ALU.mult).then_inc(v_mcol, 1)
            dve.wait_ge(a_gs, 1)
            dve.wait_ge(a_e, NT)
            link(V.tensor_tensor(esum, esum, gs, ALU.mult))
            V.tensor_reduce(zc, esum, AX.X, ALU.add).then_inc(v_z, 1)
            dve.wait_ge(t_z, 1)
            link(V.reciprocal(zr, ps[:, 1024:1025]))
            link(V.tensor_scalar(gs, gs, zr, None, ALU.mult))
            v3 = vtok[:, :].rearrange("p (t d) -> p t d", t=NT)
            V.tensor_tensor(v3, v3, gs[:, :, None].broadcast_to([P, NT, P]), ALU.mult).then_inc(v_vs, 1)
            for j in range(4):
                dve.wait_ge(t_av, j + 1)
                d = x1[:, 512 * j:512 * j + 512]
                V.scalar_tensor_tensor(out=d, in0=ps[:, 512 * j:512 * j + 512], scalar=gaf, in1=d,
                                       op0=ALU.mult, op1=ALU.add).then_inc(v_x1, 1)
            dve.wait_ge(t_x1t, 4)
            layer_stats(lambda t: ps[:, T + P * t:T + P * t + P])
            for t in range(NT):
                V.tensor_scalar(xntok[:, t, :], ps[:, T + P * t:T + P * t + P], bnmv[:, 2 * t:2 * t + 1],
                                rs16[:, t:t + 1], ALU.subtract, ALU.mult).then_inc(v_xn2, 1)

            CH = 14
            start = chained[0]

            def heads(ap):
                return ap.rearrange("p (h w d) -> p h w d", h=H, w=2)

            def rot(ap):
                return heads(ap)[:, :, ::-1, :]

            def table(u, k):
                return tabs[u][:, DH * k:DH * k + DH].rearrange("p (w d) -> p w d", w=2)[:, None, :, :]\
                    .broadcast_to([P, H, 2, DH // 2])

            def step(n, u):
                count = [0]

                def linked():
                    dve.wait_ge(v_ch, n * CH + (start + count[0]))

                def link_on(times=1):
                    for _ in range(times):
                        if count[0] > 0:
                            linked()
                        chain[count[0]]().then_inc(v_ch, 1)
                        count[0] += 1

                a_, b_, y_, x_ = nw_a[:, 0:33], nw_b[:, 0:33], nw_y[:, 0:33], nw_x[:, 0:33]
                chain = [
                    lambda: V.bn_aggr(mv2, st2) if live(n - 3) else V.memset(mv2, 0.0),
                    lambda: V.tensor_scalar(nw_x[:, 32:33], mv2[:, 1:2], LN_EPS, None, ALU.add),
                    lambda: V.tensor_scalar(nw_x[:, 0:32], nw_x[:, 0:32], NORM_EPS2, None, ALU.max)
                    if live(n) else V.memset(nw_x[:, 0:32], 1.0),
                    lambda: V.tensor_scalar(a_.bitcast(I32), x_.bitcast(I32), 1, None, ALU.logical_shift_right),
                    lambda: V.tensor_scalar(y_.bitcast(I32), a_.bitcast(I32), -1.0, float(MAGIC),
                                            ALU.mult, ALU.add),
                ]
                for k in range(3):
                    chain += [
                        lambda: V.tensor_tensor(a_, x_, y_, ALU.mult),
                        lambda: V.scalar_tensor_tensor(out=b_, in0=a_, scalar=-0.5, in1=y_,
                                                       op0=ALU.mult, op1=ALU.mult),
                        lambda k=k: V.scalar_tensor_tensor(out=rk[u] if k == 2 else y_, in0=b_, scalar=1.5,
                                                           in1=y_, op0=ALU.add, op1=ALU.mult),
                    ]
                assert len(chain) == CH
                chained_step = live(n) or live(n - 3)

                if live(n):
                    need(dve, "a_sqq", n)
                    need(dve, "g_tab", n)
                    need(dve, "t_tq", n - 1)
                    V.tensor_tensor(heads(qc), heads(pj), table(u, 0), ALU.mult)
                if live(n - 3):
                    need(dve, "t_o", n - 3)
                    need(dve, "t_to", n - 4)
                    V.tensor_copy(osb, b7[:, 0:P]).then_inc(S["v_os"], 1)
                if live(n):
                    V.tensor_tensor(heads(qsn), rot(pj), table(u, 1), ALU.mult).then_inc(S["v_qq"], 1)
                if live(n - 5):
                    need(dve, "t_w2", n - 5)
                    need(dve, "t_tf", n - 6)
                    V.tensor_copy(fsb, b6[:, 384:512]).then_inc(S["v_f"], 1)
                if live(n - 1):
                    need(dve, "t_xw", n - 1)
                    need(dve, "t_y0", n - 3)
                    V.tensor_copy(xw[1 - u], b7).then_inc(S["v_xw"], 1)
                if live(n - 5):
                    need(dve, "t_tf", n - 5)
                    need(dve, "g_xs", n - 4)
                    t5 = tile_of(n - 5)
                    V.scalar_tensor_tensor(out=xa[:, bass.ds(t5 * P + PAD, P)], in0=b6[:, 0:P],
                                           scalar=b2T[:, bass.ds(layer_of(n - 5), 1)],
                                           in1=xb[:, bass.ds(t5 * P + 1, P)], op0=ALU.add, op1=ALU.add)\
                        .then_inc(S["v_xa"], 1)
                if live(n - 2):
                    need(dve, "a_ex", n - 2)
                    need(dve, "g_pn", n - 3)
                    V.reciprocal(ri_, rsum).then_inc(S["v_ri"], 1)
                if live(n - 3):
                    need(dve, "t_to", n - 3)
                    t3 = tile_of(n - 3)
                    V.tensor_tensor(xb[:, bass.ds(t3 * P + 1, P)], b7[:, 0:P], xa[:, bass.ds(t3 * P + PAD, P)],
                                    ALU.add).then_inc(S["v_xb"], 1)
                if live(n):
                    V.tensor_reduce(nw_x[:, 0:16], sqq.rearrange("p (h d) -> p h d", h=H), AX.X, ALU.add)\
                        .then_inc(S["v_ssq"], 1)
                if live(n - 4):
                    need(dve, "t_xnt", n - 4)
                    need(dve, "t_ha", n - 5)
                    l4 = layer_of(n - 4)
                    V.tensor_scalar(xnT, b7[:, P:2 * P], lngT[:, bass.ds(l4, 1)], lnbT[:, bass.ds(l4, 1)],
                                    ALU.mult, ALU.add).then_inc(S["v_xnT"], 1)
                if live(n):
                    need(dve, "a_sqk", n)
                    need(dve, "t_tk", n - 1)
                    V.tensor_tensor(heads(kc), heads(pj), table(u, 2), ALU.mult)
                if live(n - 4):
                    need(dve, "t_hg", n - 4)
                    need(dve, "a_gel", n - 5)
                    dve.wait_ge(s_b1, (layer_of(n - 4) + 1) * 16)
                    V.tensor_tensor(gate, b6[:, 0:FI], b1b[:, bass.ds(slot_of(n - 4) * 2 * FI + FI, FI)],
                                    ALU.add).then_inc(S["v_gate"], 1)
                if live(n):
                    V.tensor_tensor(heads(ksn), rot(pj), table(u, 3), ALU.mult).then_inc(S["v_kk"], 1)
                if live(n - 4):
                    need(dve, "t_ha", n - 4)
                    need(dve, "g_h", n - 5)
                    V.tensor_tensor(ha, b6[:, 0:FI], b1b[:, bass.ds(slot_of(n - 4) * 2 * FI, FI)],
                                    ALU.add).then_inc(S["v_ha"], 1)
                if live(n - 1):
                    need(dve, "t_sc", n - 1)
                    need(dve, "a_ex", n - 2)
                    V.tensor_tensor(sm.rearrange("p (a r k) -> p r a k", r=2, k=NK),
                                    sy.rearrange("p (r a k) -> p r a k", r=2, k=NK),
                                    maskb[:, bass.ds(tile_of(n - 1) * NK, NK)][:, None, None, :]
                                    .broadcast_to([P, 2, PR, NK]), ALU.add).then_inc(S["v_ms"], 1)
                if live(n - 3):
                    need(dve, "t_x2", n - 3)
                    V.tensor_copy(x2c, b6[:, 0:P])
                    V.bn_stats(st2, b6[:, 0:P]).then_inc(S["v_bn"], 1)
                if live(n):
                    V.tensor_reduce(nw_x[:, 16:32], sqk.rearrange("p (h d) -> p h d", h=H), AX.X, ALU.add)\
                        .then_inc(S["v_ssk"], 1)
                if chained_step:
                    apart(dve)
                    need(dve, "v_bn", n - 3)
                    need(dve, "v_ssk", n)
                    need(dve, "v_ssq", n)
                    need(dve, "g_krn", n - 2)
                    link_on()
                if live(n - 1):
                    need(dve, "v_ms", n - 1)
                    V.tensor_reduce(smax, sm.rearrange("p (h k) -> p h k", h=H), AX.X, ALU.max)\
                        .then_inc(S["v_mx"], 1)
                if chained_step:
                    link_on(1)
                if live(n - 1):
                    need(dve, "v_mx", n - 1)
                    V.scalar_tensor_tensor(out=nbias[1 - u], in0=smax, scalar=-1.0, in1=q8[1 - u],
                                           op0=ALU.mult, op1=ALU.mult).then_inc(S["v_nb"], 1)
                if chained_step:
                    link_on(1)
                if live(n - 4):
                    need(dve, "t_th", n - 4)
                    need(dve, "t_w2", n - 5)
                    V.tensor_copy(hT_[:, 0:2 * P], b6[:, 0:2 * P])
                    V.tensor_copy(hT_[0:85, 2 * P:3 * P], b6[0:85, 2 * P:3 * P]).then_inc(S["v_hT"], 1)
                if chained_step:
                    link_on(CH - 3)
                    linked()
                if live(n):
                    need(dve, "a_ex", n - 2)
                    V.tensor_scalar(q8[u], rk[u][:, 0:16], 8.0, None, ALU.mult).then_inc(S["v_rs"], 1)
                if live(n - 3):
                    need(dve, "t_xnt", n - 4)
                    V.tensor_scalar(xn2, x2c, mv2[:, 0:1], rk[u][:, 32:33], ALU.subtract, ALU.mult)\
                        .then_inc(S["v_lnx"], 1)

            dve.wait_ge(s_lnp, 64)
            dve.wait_ge(s_msk, 16)
            dve.wait_ge(a_xa, 4)
            V.memset(mv2, 0.0).then_inc(S["v_xa"], NT)
            run(dve, step)

            need(dve, "v_xa", E - 1)
            for i in range(4):
                d = x1[:, 512 * i:512 * i + 512]
                V.scalar_tensor_tensor(out=d, in0=xa[:, PAD + 512 * i:PAD + 512 * i + 512], scalar=gbf, in1=d,
                                       op0=ALU.mult, op1=ALU.add).then_inc(v_fin, 1)

        @block.gpsimd
        def _(pool):
            G = nc.gpsimd
            pool.wait_ge(t_av, 4)
            G.memset(xa[:, 0:PAD], 0.0).then_inc(g_init, 1)
            G.memset(xb[:, 0:1], 0.0).then_inc(g_init, 1)
            G.memset(KT, 0.0).then_inc(g_init, 1)

            def shifted_input(e, u):
                apart(pool)
                need(pool, "g_krn", e - 2)
                need(pool, "g_tab", e - 1)
                need(pool, "g_pn", e - 4)
                need(pool, "g_h", e - 6)
                need(pool, "v_xa", e - NT)
                need(pool, "g_xd", e - 2)
                need(pool, "t_pk", e - 2)
                o = tile_of(e) * P + (PAD - W)
                G.tensor_copy(xs[u][0:64, :], xa[0:64, bass.ds(o, P + W)])
                G.tensor_copy(xs[u][64:128, :], xa[64:128, bass.ds(o - 1, P + W)]).then_inc(S["g_xs"], 1)
                need(pool, "g_xs", e)

            def window_pairs(e, u):
                apart(pool)
                need(pool, "g_xs", e)
                need(pool, "t_xw", e - 1)
                v = xs[u]
                keys = bass.AP(v.tensor, v.offset, [v.ap[0], (W, NW), (0, 2), (1, NK)])
                G.tensor_copy(xd.rearrange("p (j r k) -> p j r k", j=NW, r=2), keys).then_inc(S["g_xd"], 1)

            def scaled_tables(e, u):
                need(pool, "v_kk", e - 2)
                pool.wait_ge(s_scl, (layer_of(e) + 1) * 96)
                G.tensor_tensor(tabs[u], tabb[:, bass.ds(tile_of(e) * 4 * DH, 4 * DH)],
                                scl[:, bass.ds(slot_of(e) * 4 * DH, 4 * DH)], ALU.mult).then_inc(S["g_tab"], 1)

            def step(n, u):
                if live(n + 1):
                    shifted_input(n + 1, 1 - u)
                if live(n - 2):
                    need(pool, "a_ex", n - 2)
                    need(pool, "v_ri", n - 2)
                    p3 = pr.rearrange("p (h k) -> p h k", h=H)
                    G.tensor_tensor(p3, p3, ri_[:, :, None].broadcast_to([P, H, NK]), ALU.mult)\
                        .then_inc(S["g_pn"], 1)
                if live(n + 1):
                    scaled_tables(n + 1, 1 - u)
                if live(n):
                    window_pairs(n, u)
                if live(n - 3):
                    apart(pool)
                    need(pool, "g_tab", n + 1)
                    need(pool, "g_xd", n)
                    need(pool, "g_krn", n - 1)
                    need(pool, "g_h", n - 5)
                    need(pool, "g_pn", n - 2)
                    need(pool, "v_xb", n - 3)
                    need(pool, "t_x2", n - 4)
                    t3 = tile_of(n - 3)
                    G.tensor_copy(xs2[0:64, :], xb[0:64, bass.ds(t3 * P + 1, P)])
                    G.tensor_copy(xs2[64:128, :], xb[64:128, bass.ds(t3 * P, P)]).then_inc(S["g_xs2"], 1)
                    need(pool, "g_xs2", n - 3)
                if live(n):
                    need(pool, "v_qq", n)
                    G.tensor_tensor(qc, qc, qsn, ALU.add).then_inc(S["g_qr"], 1)
                if live(n - 4):
                    need(pool, "v_ha", n - 4)
                    need(pool, "a_gel", n - 4)
                    need(pool, "t_th", n - 5)
                    G.tensor_tensor(hh, ha, gel, ALU.mult).then_inc(S["g_h"], 1)
                if live(n):
                    need(pool, "v_kk", n)
                    G.tensor_tensor(kc, kc, ksn, ALU.add).then_inc(S["g_kr"], 1)
                if live(n):
                    need(pool, "t_sc", n - 1)
                    need(pool, "a_KT", n - 1)
                    G.tensor_tensor(KT3[:, :, 0:W], KT3[:, :, P:P + W],
                                    carry[:, :, None].broadcast_to([P, PR, W]), ALU.mult)\
                        .then_inc(S["g_kcar"], 1)
                if live(n):
                    need(pool, "v_rs", n)
                    need(pool, "g_kr", n)
                    k3 = kc.rearrange("p (h d) -> p h d", h=H)
                    G.tensor_tensor(k3, k3, rk[u][:, 16:32][:, :, None].broadcast_to([P, H, DH]), ALU.mult)\
                        .then_inc(S["g_krn"], 1)

            pool.wait_ge(a_xa, 4)
            pool.wait_ge(s_tab, 16)
            pool.wait_ge(s_lnp, 64)
            pool.wait_ge(g_init, 3)
            shifted_input(0, 0)
            scaled_tables(0, 0)
            run(pool, step, E - UNROLL)


_INS = ["L0_attn_x", "L0_attn_Wq", "L0_attn_bq", "L0_attn_Wk", "L0_attn_bk", "L0_attn_Wv", "L0_attn_bv",
        "L0_ffn_Wqkv", "L0_ffn_q_scale", "L0_ffn_k_scale", "L0_ffn_Wo", "L0_ffn_ln_g", "L0_ffn_ln_b",
        "L0_ffn_W1", "L0_ffn_b1", "L0_ffn_W2", "L0_ffn_b2", "L0_c", "L0_wmod"]


def kernel(**inputs):
    import concourse.bacc as bacc
    from concourse.bass_utils import run_bass_kernel_spmd

    nc = bacc.Bacc("TRN2", target_bir_lowering=False, num_devices=1)
    by_channel = ("L0_ffn_ln_g", "L0_ffn_ln_b", "L0_ffn_b2", "L0_c")
    arrays = {"in_" + n: np.ascontiguousarray(inputs[n].T if n in by_channel else inputs[n]) for n in _INS}
    for n, a in zip(("eye", "rotary", "mask", "diagonal", "carry"), shape_tables()):
        arrays["const_" + n] = a
    aps = [nc.dram_tensor(n, a.shape, mybir.dt.from_np(a.dtype), kind="ExternalInput").ap()
           for n, a in arrays.items()]
    out = nc.dram_tensor("out", (1, T, P), F32, kind="ExternalOutput").ap()
    program(nc, *aps, out)
    r = run_bass_kernel_spmd(nc, [arrays], core_ids=[0])
    return r.results[0]["out"]
```

```python
from contextlib import ExitStack

import numpy as np

import concourse.bass as bass
from concourse import mybir

F32 = mybir.dt.float32
I32 = mybir.dt.int32
ALU = mybir.AluOpType
ACT = mybir.ActivationFunctionType
AX = mybir.AxisListType

P = 128
T = 2048
NT = T // P
L = 6
H = 16
DH = 64
W = 32
NW = P // W
PR = H // 2
NK = 2 * W
FI = 341
FCH = [(0, 128), (128, 128), (256, 85)]
E = L * NT
BANK = 512
BIG = 1.0e30
MAGIC = 0x5F3759DF
LN_EPS = 1e-5
NORM_EPS2 = 1e-24
FILL, UNROLL = 6, 2
LAST = E + 5
STAGE = 4


def shape_tables():
    f = np.float32
    half = np.arange(0, DH, 2, dtype=f)
    inv = (f(1.0) / np.power(f(10000.0), half / f(DH))).astype(f)
    t = np.arange(T, dtype=f)
    fr = (t[:, None] * inv[None, :]).astype(f)
    fr = np.concatenate([fr, fr], -1)
    base = (half.astype(np.float64) + 0.4 * DH) / (1.4 * DH)
    sc = base[None, :] ** ((np.arange(T) % P - P // 2) / (W // 2))[:, None]
    sc = np.concatenate([sc, sc], -1)
    carry = np.tile(base ** (P / (W // 2)), P // len(base))[:, None]
    cos, sin = np.cos(fr).astype(f), np.sin(fr).astype(f)
    sgn = np.concatenate([-np.ones(DH // 2, f), np.ones(DH // 2, f)])
    iv = 1.0 / sc
    tab = np.stack([cos * sc, sin * sgn * sc, cos * iv, sin * sgn * iv], 1).astype(f)
    tab = tab.reshape(NT, P, 4 * DH).transpose(1, 0, 2).reshape(P, NT * 4 * DH)
    q = np.arange(P)
    i, j = (q % W)[:, None], np.arange(NK)[None, :]
    m = np.where((j >= i) & (j <= i + W), 0.0, -BIG)
    mask = np.repeat(m[:, None, :], NT, 1)
    mask[:W, 0, :W] = -BIG
    diag = np.where(q[None, :] >= q[:, None], 0.0, -BIG)
    return [np.ascontiguousarray(a, f) for a in (np.eye(P), tab, mask.reshape(P, NT * NK), diag, carry)]


def program(nc, x, wq, bq, wk, bk, wv, bv, wqkv, qs, ks, wo, lng, lnb, w1, b1, w2, b2, c, wmod,
            eye, tab, maskt, diagt, carryt, out):
    SCALE = float(P) ** -0.5
    ctx = ExitStack()
    with ctx:
        def sb(name, *shape, dt=F32):
            return ctx.enter_context(nc.sbuf_tensor(name, [P, *shape], dt))

        def sem(name):
            return ctx.enter_context(nc.semaphore(name))

        ident = sb("ident", P)
        diag = sb("diag", P)
        maskb = sb("maskb", NT * NK)
        tabb = sb("tabb", NT * 4 * DH)
        wqk = sb("wqk", 2 * 2048)
        w1b = sb("w1b", 2 * 2 * FI)
        b1b = sb("b1b", 2 * 2 * FI)
        w2b = sb("w2b", 2 * 3 * P)
        scl = sb("scl", 2 * 4 * DH)
        wvo = sb("wvo", L * H * P)
        PAD = W + 1
        xa = sb("xa", PAD + T)
        xb = sb("xb", 1 + T)
        x1 = sb("x1", T)
        vtok = sb("vtok", T)
        arena = sb("arena", 136 * P)
        small = sb("small", 1024)
        at = [0]

        def cols(n):
            at[0] += n
            return small[:, at[0] - n:at[0]]

        ccol, sig, silu = cols(1), cols(1), cols(1)
        modT, ca1, cb1, gaf, gbf, tmpa, tmpb = cols(6), cols(1), cols(1), cols(1), cols(1), cols(2), cols(2)
        bqc, bkc = cols(1), cols(1)
        bvr = cols(P)
        bnst, bnmv, rs16 = cols(6 * NT), cols(2 * NT), cols(NT)
        mx, negm, esum, gs, zc, zr, mcol = cols(NT), cols(NT), cols(NT), cols(NT), cols(1), cols(1), cols(1)
        mrow, ones = cols(P), cols(P)
        lngT, lnbT, b2T = cols(L), cols(L), cols(L)
        nw_x, nw_y, nw_a, nw_b = cols(33), cols(33), cols(33), cols(33)
        ri_, carry = cols(16), cols(1)
        st2, mv2 = cols(6), cols(2)
        rk = [cols(33), cols(33)]
        q8 = [cols(16), cols(16)]
        smax, rsum, dummy = cols(16), cols(16), cols(2)

        wmod_s = arena[:, 0:768]
        wq_s, wk_s, wv_s = arena[:, 768:896], arena[:, 896:1024], arena[:, 1024:1152]
        xtok = arena[:, 2048:4096].rearrange("p (t d) -> p t d", t=NT)
        xntok = arena[:, 4096:6144].rearrange("p (t d) -> p t d", t=NT)
        wv_st = [arena[:, 6144 + 1024 * i:7168 + 1024 * i] for i in range(STAGE)]
        wo_st = [arena[:, 10240 + 1024 * i:11264 + 1024 * i] for i in range(STAGE)]
        wvT = [arena[:, 14336 + 1024 * i:15360 + 1024 * i] for i in range(2)]
        hT, qT0, kT0 = xa[:, 0:T], xb[:, 0:T], wqk[:, 2048:4096]
        eoff = [0]
        for s in range(NT):
            eoff.append(eoff[-1] + T - P * s)

        off = [0]

        def buf(n):
            off[0] += n
            return arena[:, off[0] - n:off[0]]

        xs = [buf(P + W), buf(P + W)]
        xd = buf(NW * 2 * NK)
        xw = [buf(NW * P), buf(NW * P)]
        tabs = [buf(4 * DH), buf(4 * DH)]
        sqq, sqk = buf(1024), buf(1024)
        qc, qsn, kc, ksn = buf(1024), buf(1024), buf(1024), buf(1024)
        QT, KT = buf(1024), buf(PR * (P + W))
        sm, pr, pT = buf(1024), buf(1024), buf(1024)
        ysb = [buf(1024), buf(1024)]
        osb, xs2, xn2, xnT, x2c = buf(P), buf(P), buf(P), buf(P), buf(P)
        gate, gel, ha, hh = (vtok[:, FI * i:FI * i + FI] for i in range(4))
        hT_, fsb = vtok[:, 4 * FI:4 * FI + 3 * P], vtok[:, 4 * FI + 3 * P:4 * FI + 4 * P]
        QT3 = QT.rearrange("p (a t) -> p a t", a=PR)
        KT3 = KT.rearrange("p (a t) -> p a t", a=PR)
        pT3 = pT.rearrange("p (a t) -> p a t", a=PR)

        ps = ctx.enter_context(nc.psum_tensor("ps", [P, 8 * BANK], F32))
        pj = ps[:, 0:1024]
        tp = ps[:, 1024:2048]
        sy = ps[:, 2048:3072]
        b6 = ps[:, 3072:3584]
        b7 = ps[:, 3584:4096]

        s_x, s_cw, s_wl = sem("s_x"), sem("s_cw"), sem("s_wl")
        s_id, s_wqk, s_w1, s_b1, s_w2 = sem("s_id"), sem("s_wqk"), sem("s_w1"), sem("s_b1"), sem("s_w2")
        s_scl, s_tab, s_msk, s_lnp = sem("s_scl"), sem("s_tab"), sem("s_msk"), sem("s_lnp")
        s_wst = [sem("s_wst%d" % i) for i in range(STAGE)]
        s_out = sem("s_out")
        v_ch = sem("v_ch")
        a_sig, v_silu, t_mod, v_mod = sem("a_sig"), sem("v_silu"), sem("t_mod"), sem("v_mod")
        v_xn, t_xT, t_xnT, a_x1, a_hT = sem("v_xn"), sem("t_xT"), sem("t_xnT"), sem("a_x1"), sem("a_hT")
        t_q, t_k, t_v, a_qk, v_v = sem("t_q"), sem("t_k"), sem("t_v"), sem("a_qk"), sem("v_v")
        t_wvT, a_wvT, t_m, a_m = sem("t_wvT"), sem("a_wvT"), sem("t_m"), sem("a_m")
        t_s, v_nm, a_e = sem("t_s"), sem("v_nm"), sem("a_e")
        t_mr, v_mrow, t_mc, v_mcol, a_gs, v_z, t_z, v_vs = (sem("t_mr"), sem("v_mrow"), sem("t_mc"), sem("v_mcol"),
                                                    sem("a_gs"), sem("v_z"), sem("t_z"), sem("v_vs"))
        t_av, v_x1, t_x1t, v_xn2, t_x2T, a_xa = (sem("t_av"), sem("v_x1"), sem("t_x1t"), sem("v_xn2"),
                                                 sem("t_x2T"), sem("a_xa"))
        g_init = sem("g_init")
        v_fin, t_fin, a_fin = sem("v_fin"), sem("t_fin"), sem("a_fin")
        names = ("g_h g_tab g_qr g_kr g_krn g_sub g_sq g_pn "
                 "t_tq t_tk t_xw t_pq t_pk t_sc t_pT t_y0 t_y1 t_o t_to t_x2 t_xnt t_hg t_ha t_th t_w2 t_tf "
                 "a_sqq a_sqk a_QT a_KT a_ex a_pT a_y0 a_y1 a_gel a_xs a_xd a_xs2 a_xw a_os a_f a_hd a_xnT a_kcar "
                 "v_xb v_qq v_xa v_ssq v_ms v_mx v_bn v_kk v_ssk v_gate v_ha v_rs v_lnx v_sum v_ri")
        S = {n: sem("p" + n) for n in names.split()}

        block = ctx.enter_context(nc.Block())

        def need(eng, name, e):
            if isinstance(e, int):
                e = min(e, E - 1)
                if e + ahead.get(name, 0) < 0:
                    return
            eng.wait_ge(S[name], e + (ahead.get(name, 0) + 1))

        ahead = {"v_xa": NT}

        def apart(eng):
            eng.wait_ge(s_id, 16)

        def live(e):
            return not isinstance(e, int) or 0 <= e < E

        def run(eng, step, end=E):
            for n in range(FILL):
                step(n, n % 2)
            with eng.Fori(FILL, end, UNROLL) as i:
                for u in range(UNROLL):
                    step(i + u, u)
            for n in range(end, LAST):
                step(n, n % 2)

        def tile_of(e):
            return e % NT

        def layer_of(e):
            return e // NT

        def slot_of(e):
            return (e // NT) % 2

        @block.sync
        def _(sp):
            sp.dma_start(xtok, x[0].rearrange("(t p) d -> p t d", p=P)).then_inc(s_x, 16)
            sp.dma_start(ident[:, :], eye).then_inc(s_id, 16)
            sp.dma_start(ccol, c).then_inc(s_cw, 16)
            sp.dma_start(wmod_s, wmod).then_inc(s_cw, 16)
            sp.dma_start(wq_s, wq).then_inc(s_wl, 16)
            sp.dma_start(wk_s, wk).then_inc(s_wl, 16)
            sp.dma_start(wv_s, wv).then_inc(s_wl, 16)
            sp.dma_start(bqc, bq.rearrange("(d a) -> d a", a=1)).then_inc(s_wl, 16)
            sp.dma_start(bkc, bk.rearrange("(d a) -> d a", a=1)).then_inc(s_wl, 16)
            sp.dma_start(bvr, bv.partition_broadcast(P)).then_inc(s_wl, 16)
            sp.dma_start(diag[:, :], diagt).then_inc(s_wl, 16)
            for l in range(L):
                if l >= STAGE:
                    sp.wait_ge(t_m, 2 * (l - STAGE + 1))
                sp.dma_start(wv_st[l % STAGE], wqkv[l, :, 2048:3072]).then_inc(s_wst[l % STAGE], 16)
                sp.dma_start(wo_st[l % STAGE].rearrange("p (a d) -> p a d", a=PR),
                             wo[l].rearrange("(a p) d -> p a d", p=P)).then_inc(s_wst[l % STAGE], 16)
            sp.dma_start(maskb[:, :], maskt).then_inc(s_msk, 16)
            sp.dma_start(tabb[:, :], tab).then_inc(s_tab, 16)
            sp.dma_start(carry, carryt).then_inc(s_lnp, 16)
            sp.dma_start(lngT, lng).then_inc(s_lnp, 16)
            sp.dma_start(lnbT, lnb).then_inc(s_lnp, 16)
            sp.dma_start(b2T, b2).then_inc(s_lnp, 16)

            def layer_weights(l):
                o = (l % 2)
                def dst(t, n):
                    return t[:, bass.ds(o * n, n)]
                sp.dma_start(dst(wqk, 2048), wqkv[l, :, 0:2048]).then_inc(s_wqk, 16)
                sp.dma_start(dst(w1b, 2 * FI), w1[l]).then_inc(s_w1, 16)
                sp.dma_start(dst(b1b, 2 * FI), b1[l].partition_broadcast(P)).then_inc(s_b1, 16)
                w2d = dst(w2b, 3 * P)
                for j, (k0, kn) in enumerate(FCH):
                    sp.dma_start(w2d[0:kn, j * P:(j + 1) * P], w2[l, k0:k0 + kn, :]).then_inc(s_w2, 16)
                for j, (r, lo) in enumerate(((qs, 0), (qs, 1), (ks, 0), (ks, 1))):
                    sd = dst(scl, 4 * DH)
                    if lo == 0:
                        sp.dma_start(sd[:, j * DH:(j + 1) * DH], r[l].partition_broadcast(P)).then_inc(s_scl, 16)
                    else:
                        for a in range(2):
                            sp.dma_start(sd[:, j * DH + 32 * a:j * DH + 32 * a + 32],
                                         r[l, 32 - 32 * a:64 - 32 * a].partition_broadcast(P)).then_inc(s_scl, 16)

            layer_weights(0)
            sp.wait_ge(t_s, NT)
            for s_, v_ in ((s_wqk, 16), (s_w1, 16), (s_b1, 16), (s_w2, 48), (s_scl, 96)):
                sp.wait_ge(s_, v_)
            layer_weights(1)
            with sp.Fori(2, L) as l:
                through = sp.snap(l * NT - (NT - 1))
                apart(sp)
                sp.wait_ge(S["t_w2"], through)
                layer_weights(l)
            for i in range(4):
                sp.wait_ge(a_fin, i + 1)
                sp.dma_start(out[0, 512 * i:512 * i + 512].rearrange("(t p) d -> p t d", p=P),
                             xtok[:, 4 * i:4 * i + 4, :]).then_inc(s_out, 16)
            sp.wait_ge(s_out, 64)

        @block.tensor
        def _(pe):
            mm = nc.tensor.matmul

            def tr(o, i, n=P):
                return nc.tensor.transpose(o, i, ident[0:n, 0:n])

            pe.wait_ge(s_cw, 32)
            pe.wait_ge(v_silu, 1)
            for j in range(6):
                last = mm(b7[:, j:j + 1], wmod_s[:, j * P:(j + 1) * P], silu, start=True, stop=True)
            last.then_inc(t_mod, 1)
            pe.wait_ge(s_x, 16)
            pe.wait_ge(s_id, 16)
            for t in range(NT):
                last = tr(ps[:, P * t:P * t + P], xtok[:, t, :])
                if t % 4 == 3:
                    last.then_inc(t_xT, 1)
            pe.wait_ge(v_mod, 1)
            for t in range(NT):
                if t % 4 == 0:
                    pe.wait_ge(v_xn, t + 4)
                last = tr(ps[:, T + P * t:T + P * t + P], xntok[:, t, :])
                if t % 4 == 3:
                    last.then_inc(t_xnT, 1)
            pe.wait_ge(s_wl, 112)
            for j in range(4):
                pe.wait_ge(a_x1, j + 1)
                pe.wait_ge(a_hT, j + 1)
                mm(ps[:, 512 * j:512 * j + 512], wq_s, hT[:, 512 * j:512 * j + 512],
                   start=True, stop=True).then_inc(t_q, 1)
            for j in range(4):
                mm(ps[:, T + 512 * j:T + 512 * j + 512], wk_s, hT[:, 512 * j:512 * j + 512],
                   start=True, stop=True).then_inc(t_k, 1)
            for t in range(NT):
                if t % 4 == 0:
                    pe.wait_ge(a_qk, t // 4 + 1)
                last = mm(ps[:, P * t:P * t + P], hT[:, P * t:P * t + P], wv_s, start=True, stop=True)
                if t % 4 == 3:
                    last.then_inc(t_v, 1)
            def wv_transposes(l):
                pe.wait_ge(s_wst[l % STAGE], 32 * (l // STAGE + 1))
                if l >= 2:
                    pe.wait_ge(a_wvT, l - 1)
                for p in range(PR):
                    last = tr(ps[:, 1024 * (l % 2) + P * p:1024 * (l % 2) + P * p + P],
                              wv_st[l % STAGE][:, P * p:P * p + P])
                last.then_inc(t_wvT, 1)

            pe.wait_ge(v_v, 4)
            pe.wait_ge(a_qk, 8)
            wv_transposes(0)
            for l in range(L):
                if l + 1 < L:
                    wv_transposes(l + 1)
                pe.wait_ge(a_wvT, l + 1)
                for r in range(2):
                    if l:
                        pe.wait_ge(a_m, 2 * (l - 1) + r + 1)
                    for p in range(PR):
                        last = mm(ps[:, T + 1024 * r + P * p:T + 1024 * r + P * p + P],
                                  wvT[l % 2][DH * r:DH * r + DH, P * p:P * p + P],
                                  wo_st[l % STAGE][DH * r:DH * r + DH, P * p:P * p + P], start=True, stop=True)
                    last.then_inc(t_m, 1)
            pe.wait_ge(a_m, 2 * L)
            for s in range(NT):
                base = T * (s % 2)
                if s >= 2:
                    pe.wait_ge(a_e, s - 1)
                for j in range(s // 4, 4):
                    lo = max(512 * j, P * s)
                    last = mm(ps[:, base + lo:base + 512 * j + 512], kT0[:, P * s:P * s + P],
                              qT0[:, lo:512 * j + 512], start=True, stop=True)
                last.then_inc(t_s, 1)
            pe.wait_ge(v_mrow, 1)
            tr(ps[0:1, 0:P], mcol).then_inc(t_mr, 1)
            pe.wait_ge(v_mrow, 2)
            mm(ps[:, 512:513], ones[0:1, :], mrow[0:1, 0:1], start=True, stop=True).then_inc(t_mc, 1)
            pe.wait_ge(v_z, 1)
            mm(ps[:, 1024:1025], ones, zc, start=True, stop=True).then_inc(t_z, 1)
            pe.wait_ge(v_vs, 1)
            def to_tokens(j):
                pe.wait_ge(v_x1, j + 1)
                for t in range(4 * j, 4 * j + 4):
                    last = tr(ps[:, T + P * t:T + P * t + P], x1[:, P * t:P * t + P])
                last.then_inc(t_x1t, 1)

            def to_channels(j):
                pe.wait_ge(v_xn2, 4 * j + 4)
                for t in range(4 * j, 4 * j + 4):
                    last = tr(ps[:, P * t:P * t + P], xntok[:, t, :])
                last.then_inc(t_x2T, 1)

            for j in range(4):
                for s in range(4 * j + 4):
                    lo = max(512 * j, P * s)
                    last = mm(ps[:, lo:512 * j + 512], vtok[:, P * s:P * s + P],
                              arena[:, eoff[s] + lo - P * s:eoff[s] + 512 * j + 512 - P * s],
                              start=(s == 0), stop=(s == 4 * j + 3))
                    if j and s == 3:
                        to_tokens(j - 1)
                last.then_inc(t_av, 1)
            to_tokens(3)
            for j in range(4):
                to_channels(j)

            def project(n, u, part, j):
                return mm(pj[:, 512 * j:512 * j + 512], xs[u][:, W:],
                          wqk[:, bass.ds(slot_of(n) * 2048 + (1024 * part + 512 * j), 512)],
                          start=True, stop=True)

            def scores(pairs):
                for p in pairs:
                    for j in range(NW):
                        for r in range(2):
                            last = mm(sy[W * j:W * j + W, 512 * r + NK * p:512 * r + NK * p + NK],
                                      QT3[DH * r:DH * r + DH, p, W * j:W * j + W],
                                      KT3[DH * r:DH * r + DH, p, W * j:W * j + NK], start=True, stop=True)
                return last

            def values(u, r, o):
                for j in range(NW):
                    last = mm(o[:, 256 * j:256 * j + 256].rearrange("p (a q) -> p a q", a=PR),
                              xw[u][DH * r:DH * r + DH, P * j:P * j + P],
                              pT3[DH * r:DH * r + DH, :, W * j:W * j + W], start=True, stop=True)
                return last

            def output(e, r, pairs):
                for p in pairs:
                    last = mm(b7[:, 0:P], ysb[r][:, P * p:P * p + P],
                              wvo[:, bass.ds(layer_of(e) * (H * P) + (r * PR + p) * P, P)],
                              start=(r == 1 and p == 0), stop=(r == 0 and p == PR - 1))
                return last

            def step(n, u):
                if live(n - 3):
                    need(pe, "a_y0", n - 3)
                    output(n - 3, 0, range(0, 5))
                if live(n):
                    need(pe, "a_xs", n)
                    need(pe, "a_sqk", n - 1)
                    need(pe, "v_kk", n - 1)
                    pe.wait_ge(s_wqk, (layer_of(n) + 1) * 16)
                    project(n, u, 0, 0)
                    project(n, u, 0, 1).then_inc(S["t_pq"], 1)
                if live(n - 1):
                    need(pe, "g_krn", n - 1)
                    need(pe, "a_QT", n - 1)
                    for p in range(PR):
                        last = tr(tp[:, P * p:P * p + P], kc[:, P * p:P * p + P])
                    last.then_inc(S["t_tk"], 1)
                if live(n - 5):
                    need(pe, "a_hd", n - 5)
                    pe.wait_ge(s_w2, (layer_of(n - 5) + 1) * 48)
                    for j, (k0, kn) in enumerate(FCH):
                        last = mm(b6[:, 384:512], hT_[0:kn, P * j:P * j + P],
                                  w2b[0:kn, bass.ds(slot_of(n - 5) * 3 * P + P * j, P)],
                                  start=(j == 0), stop=(j == 2))
                    last.then_inc(S["t_w2"], 1)
                if live(n - 3):
                    output(n - 3, 0, range(5, PR)).then_inc(S["t_o"], 1)
                if live(n - 1):
                    apart(pe)
                    need(pe, "a_KT", n - 1)
                    need(pe, "a_kcar", n - 1)
                    need(pe, "a_y0", n - 3)
                    scores(range(0, 4))
                if live(n - 5):
                    need(pe, "a_f", n - 5)
                    tr(b6[:, 0:P], fsb).then_inc(S["t_tf"], 1)
                if live(n - 3):
                    need(pe, "a_os", n - 3)
                    tr(b7[:, 0:P], osb).then_inc(S["t_to"], 1)
                if live(n):
                    need(pe, "a_sqq", n)
                    need(pe, "v_qq", n)
                    project(n, u, 1, 0)
                    project(n, u, 1, 1).then_inc(S["t_pk"], 1)
                if live(n - 1):
                    scores(range(4, 5))
                if live(n - 4):
                    need(pe, "v_lnx", n - 4)
                    need(pe, "v_xb", n - 3)
                    tr(b7[:, P:2 * P], xn2).then_inc(S["t_xnt"], 1)
                if live(n - 1):
                    scores(range(5, 6))
                if live(n - 2):
                    need(pe, "g_pn", n - 2)
                    need(pe, "a_KT", n - 1)
                    for p in range(PR):
                        last = tr(tp[:, P * p:P * p + P], pr[:, P * p:P * p + P])
                    last.then_inc(S["t_pT"], 1)
                if live(n - 1):
                    scores(range(6, 8)).then_inc(S["t_sc"], 1)
                if live(n - 4):
                    need(pe, "a_xnT", n - 4)
                    need(pe, "v_xa", n - 5)
                    pe.wait_ge(s_w1, (layer_of(n - 4) + 1) * 16)
                    mm(b6[:, 0:FI], xnT, w1b[:, bass.ds(slot_of(n - 4) * 2 * FI + FI, FI)],
                       start=True, stop=True).then_inc(S["t_hg"], 1)
                if live(n - 3):
                    need(pe, "a_xs2", n - 3)
                    need(pe, "a_xnT", n - 4)
                    tr(b7[:, 2 * P:3 * P], xs2).then_inc(S["t_x2"], 1)
                if live(n - 2):
                    need(pe, "a_pT", n - 2)
                    need(pe, "a_xw", n - 2)
                    values(u, 1, tp).then_inc(S["t_y1"], 1)
                if live(n - 4):
                    need(pe, "v_gate", n - 4)
                    mm(b6[:, 0:FI], xnT, w1b[:, bass.ds(slot_of(n - 4) * 2 * FI, FI)],
                       start=True, stop=True).then_inc(S["t_ha"], 1)
                if live(n - 1):
                    need(pe, "a_xd", n - 1)
                    need(pe, "v_bn", n - 3)
                    need(pe, "a_xnT", n - 4)
                    for j in range(NW):
                        last = tr(b7[:, P * j:P * j + P], xd[:, P * j:P * j + P])
                    last.then_inc(S["t_xw"], 1)
                if live(n - 2):
                    need(pe, "v_ms", n - 1)
                    values(u, 0, sy).then_inc(S["t_y0"], 1)
                if live(n):
                    need(pe, "g_qr", n)
                    need(pe, "a_y1", n - 2)
                    for p in range(PR):
                        last = tr(tp[:, P * p:P * p + P], qc[:, P * p:P * p + P])
                    last.then_inc(S["t_tq"], 1)
                if live(n - 2):
                    need(pe, "a_xw", n - 1)
                    need(pe, "v_bn", n - 3)
                    need(pe, "a_y1", n - 2)
                    output(n - 2, 1, range(PR))
                if live(n - 4):
                    need(pe, "g_h", n - 4)
                    need(pe, "v_ha", n - 4)
                    for j, (k0, kn) in enumerate(FCH):
                        last = tr(b6[0:kn, P * j:P * j + P], hh[:, k0:k0 + kn])
                    last.then_inc(S["t_th"], 1)

            pe.wait_ge(a_xa, 4)
            pe.wait_ge(g_init, 3)
            run(pe, step)

            for i in range(4):
                pe.wait_ge(v_fin, i + 1)
                for t in range(4 * i, 4 * i + 4):
                    last = tr(ps[:, P * t:P * t + P], x1[:, P * t:P * t + P])
                last.then_inc(t_fin, 1)

        @block.scalar
        def _(act):
            A = nc.scalar.activation

            def heads_first(ap):
                return ap.rearrange("d (a j q) -> d j a q", j=NW, a=PR)

            def by_window(ap):
                return ap.rearrange("d (j a q) -> d j a q", j=NW, a=PR)

            act.wait_ge(s_cw, 32)
            A(sig, ccol, ACT.Exp, scale=-1.0).then_inc(a_sig, 1)
            for j in range(4):
                act.wait_ge(t_xT, j + 1)
                A(x1[:, 512 * j:512 * j + 512], ps[:, 512 * j:512 * j + 512], ACT.Copy).then_inc(a_x1, 1)
            act.wait_ge(v_mod, 1)
            for j in range(4):
                act.wait_ge(t_xnT, j + 1)
                A(hT[:, 512 * j:512 * j + 512], ps[:, T + 512 * j:T + 512 * j + 512], ACT.Identity,
                  scale=ca1, bias=modT[:, 0:1]).then_inc(a_hT, 1)
            act.wait_ge(s_wl, 112)
            for j in range(4):
                act.wait_ge(t_q, j + 1)
                A(qT0[:, 512 * j:512 * j + 512], ps[:, 512 * j:512 * j + 512], ACT.Identity,
                  bias=bqc).then_inc(a_qk, 1)
            for j in range(4):
                act.wait_ge(t_k, j + 1)
                A(kT0[:, 512 * j:512 * j + 512], ps[:, T + 512 * j:T + 512 * j + 512], ACT.Identity,
                  bias=bkc).then_inc(a_qk, 1)
            act.wait_ge(t_wvT, 1)
            A(wvT[0], ps[:, 0:1024], ACT.Copy).then_inc(a_wvT, 1)
            for l in range(L):
                if l + 1 < L:
                    act.wait_ge(t_wvT, l + 2)
                    if l:
                        act.wait_ge(t_m, 2 * l)
                    k = (l + 1) % 2
                    A(wvT[k], ps[:, 1024 * k:1024 * k + 1024], ACT.Copy).then_inc(a_wvT, 1)
                for r in range(2):
                    act.wait_ge(t_m, 2 * l + r + 1)
                    A(wvo[:, (2 * l + r) * PR * P:(2 * l + r + 1) * PR * P], ps[:, T + 1024 * r:T + 1024 * r + 1024],
                      ACT.Copy).then_inc(a_m, 1)
            act.wait_ge(v_v, 4)
            for s in range(NT):
                act.wait_ge(v_nm, s + 1)
                base = T * (s % 2)
                A(arena[:, eoff[s]:eoff[s + 1]], ps[:, base + P * s:base + T], ACT.Exp,
                  scale=SCALE, bias=negm[:, s:s + 1], accum_out=esum[:, s:s + 1]).then_inc(a_e, 1)
            act.wait_ge(v_mcol, 1)
            A(gs, mx, ACT.Exp, scale=SCALE, bias=mcol).then_inc(a_gs, 1)
            act.wait_ge(g_init, 3)
            for j in range(4):
                act.wait_ge(t_x2T, j + 1)
                A(xa[:, PAD + 512 * j:PAD + 512 * j + 512], ps[:, 512 * j:512 * j + 512], ACT.Identity,
                  scale=cb1, bias=modT[:, 3:4]).then_inc(a_xa, 1)

            def shifted_input(e, u):
                need(act, "v_xa", e - NT)
                need(act, "a_xd", e - 2)
                need(act, "t_pk", e - 2)
                o = tile_of(e) * P + (PAD - W)
                A(xs[u][0:64, :], xa[0:64, bass.ds(o, P + W)], ACT.Copy)
                A(xs[u][64:128, :], xa[64:128, bass.ds(o - 1, P + W)], ACT.Copy).then_inc(S["a_xs"], 1)

            def step(n, u):
                if live(n - 1):
                    need(act, "t_tk", n - 1)
                    need(act, "a_kcar", n - 1)
                    A(KT3[:, :, W:], tp.rearrange("p (a t) -> p a t", a=PR), ACT.Copy).then_inc(S["a_KT"], 1)
                if live(n - 5):
                    need(act, "t_w2", n - 5)
                    need(act, "t_tf", n - 6)
                    A(fsb, b6[:, 384:512], ACT.Copy).then_inc(S["a_f"], 1)
                if live(n - 3):
                    need(act, "t_o", n - 3)
                    need(act, "t_to", n - 4)
                    A(osb, b7[:, 0:P], ACT.Copy).then_inc(S["a_os"], 1)
                if live(n):
                    need(act, "v_qq", n)
                    need(act, "v_ssq", n - 1)
                    A(sqq, pj, ACT.Square).then_inc(S["a_sqq"], 1)
                if live(n + 1):
                    shifted_input(n + 1, 1 - u)
                if live(n - 4):
                    A(dummy[:, 0:1], ones[:, 0:1], ACT.Gelu)
                if live(n - 3):
                    need(act, "v_xb", n - 3)
                    need(act, "t_x2", n - 4)
                    t3 = tile_of(n - 3)
                    A(xs2[0:64, :], xb[0:64, bass.ds(t3 * P + 1, P)], ACT.Copy)
                    A(xs2[64:128, :], xb[64:128, bass.ds(t3 * P, P)], ACT.Copy).then_inc(S["a_xs2"], 1)
                if live(n - 4):
                    need(act, "t_xnt", n - 4)
                    need(act, "t_ha", n - 5)
                    l4 = layer_of(n - 4)
                    A(xnT, b7[:, P:2 * P], ACT.Identity, scale=lngT[:, bass.ds(l4, 1)],
                      bias=lnbT[:, bass.ds(l4, 1)]).then_inc(S["a_xnT"], 1)
                if live(n - 2):
                    need(act, "t_pT", n - 2)
                    need(act, "t_y0", n - 3)
                    A(pT, tp, ACT.Copy).then_inc(S["a_pT"], 1)
                if live(n):
                    need(act, "v_kk", n)
                    need(act, "v_ssk", n - 1)
                    A(sqk, pj, ACT.Square).then_inc(S["a_sqk"], 1)
                if live(n):
                    need(act, "t_sc", n - 1)
                    need(act, "a_KT", n - 1)
                    A(KT3[:, :, 0:W], KT3[:, :, P:P + W], ACT.Copy, scale=carry).then_inc(S["a_kcar"], 1)
                if live(n - 4):
                    need(act, "v_gate", n - 4)
                    need(act, "g_h", n - 5)
                    A(gel, gate, ACT.Gelu).then_inc(S["a_gel"], 1)
                if live(n - 2):
                    need(act, "t_y1", n - 2)
                    need(act, "t_o", n - 3)
                    A(heads_first(ysb[1]), by_window(tp), ACT.Copy).then_inc(S["a_y1"], 1)
                if live(n - 1):
                    need(act, "t_xw", n - 1)
                    need(act, "t_y0", n - 3)
                    A(xw[1 - u], b7, ACT.Copy).then_inc(S["a_xw"], 1)
                if live(n):
                    need(act, "a_xs", n)
                    need(act, "t_xw", n - 1)
                    v = xs[u]
                    keys = bass.AP(v.tensor, v.offset, [v.ap[0], (W, NW), (0, 2), (1, NK)])
                    A(xd.rearrange("p (j r k) -> p j r k", j=NW, r=2), keys, ACT.Copy).then_inc(S["a_xd"], 1)
                if live(n - 1):
                    A(dummy[:, 1:2], ones[:, 0:1], ACT.Exp)
                if live(n - 2):
                    need(act, "t_y0", n - 2)
                    A(heads_first(ysb[0]), by_window(sy), ACT.Copy).then_inc(S["a_y0"], 1)
                if live(n):
                    need(act, "t_tq", n)
                    need(act, "t_sc", n - 1)
                    A(QT, tp, ACT.Copy).then_inc(S["a_QT"], 1)
                if live(n - 1):
                    need(act, "g_sq", n - 1)
                    need(act, "t_pT", n - 2)
                    A(pr, sm, ACT.Exp).then_inc(S["a_ex"], 1)
                if live(n - 4):
                    need(act, "t_th", n - 4)
                    need(act, "t_w2", n - 5)
                    A(hT_[:, 0:2 * P], b6[:, 0:2 * P], ACT.Copy)
                    A(hT_[0:85, 2 * P:3 * P], b6[0:85, 2 * P:3 * P], ACT.Copy).then_inc(S["a_hd"], 1)

            act.wait_ge(s_lnp, 64)
            act.wait_ge(g_init, 3)
            shifted_input(0, 0)
            run(act, step, E - UNROLL)
            for i in range(4):
                act.wait_ge(t_fin, i + 1)
                A(arena[:, 2048 + 512 * i:2560 + 512 * i], ps[:, 512 * i:512 * i + 512], ACT.Copy).then_inc(a_fin, 1)

        @block.vector
        def _(dve):
            V = nc.vector
            chained = [0]

            def rsqrt(k, x_, y_, done):
                a_, b_ = nw_a[:, 0:k], nw_b[:, 0:k]
                yield V.tensor_scalar(a_.bitcast(I32), x_.bitcast(I32), 1, None, ALU.logical_shift_right)
                yield V.tensor_scalar(nw_y[:, 0:k].bitcast(I32), a_.bitcast(I32), -1.0, float(MAGIC),
                                      ALU.mult, ALU.add)
                src = nw_y[:, 0:k]
                for i in range(3):
                    yield V.tensor_tensor(a_, x_, src, ALU.mult)
                    yield V.scalar_tensor_tensor(out=b_, in0=a_, scalar=-0.5, in1=src, op0=ALU.mult, op1=ALU.mult)
                    dst = y_ if i == 2 else nw_y[:, 0:k]
                    r = V.scalar_tensor_tensor(out=dst, in0=b_, scalar=1.5, in1=src, op0=ALU.add, op1=ALU.mult)
                    if i < 2:
                        yield r
                    else:
                        done(r)

            def link(ins):
                chained[0] += 1
                ins.then_inc(v_ch, 1)
                dve.wait_ge(v_ch, chained[0])

            dve.wait_ge(a_sig, 1)
            link(V.tensor_scalar(sig, sig, 1.0, None, ALU.add))
            link(V.reciprocal(silu, sig))
            V.tensor_tensor(silu, silu, ccol, ALU.mult).then_inc(v_silu, 1)
            link(V.memset(ones, 1.0))
            dve.wait_ge(s_x, 16)

            def layer_stats(src, tiles):
                a, b = tiles[0], tiles[-1] + 1
                for t in tiles:
                    last = V.bn_stats(bnst[:, 6 * t:6 * t + 6], src(t))
                link(last)
                for t in tiles:
                    last = V.bn_aggr(bnmv[:, 2 * t:2 * t + 2], bnst[:, 6 * t:6 * t + 6])
                link(last)
                var = bnmv.rearrange("p (t k) -> p t k", k=2)[:, a:b, 1]
                link(V.tensor_scalar(nw_x[:, 0:b - a], var, LN_EPS, None, ALU.add))
                for r in rsqrt(b - a, nw_x[:, 0:b - a], rs16[:, a:b], link):
                    link(r)

            layer_stats(lambda t: xtok[:, t, :], range(NT))
            for t in range(NT):
                V.tensor_scalar(xntok[:, t, :], xtok[:, t, :], bnmv[:, 2 * t:2 * t + 1], rs16[:, t:t + 1],
                                ALU.subtract, ALU.mult).then_inc(v_xn, 1)
            dve.wait_ge(t_mod, 1)
            link(V.tensor_copy(modT, b7[:, 0:6]))
            link(V.tensor_scalar(ca1, modT[:, 1:2], 1.0, None, ALU.add))
            link(V.tensor_scalar(cb1, modT[:, 4:5], 1.0, None, ALU.add))
            gates = modT.rearrange("p (k j) -> p k j", j=3)[:, :, 2]
            link(V.scalar_tensor_tensor(out=tmpa, in0=gates, scalar=-1.0, in1=gates, op0=ALU.mult, op1=ALU.max))
            link(V.tensor_scalar(tmpa, tmpa, 0.25, None, ALU.max))
            link(V.tensor_scalar(tmpb, gates, 0.0, 2.0, ALU.is_ge, ALU.mult))
            link(V.scalar_tensor_tensor(out=gaf, in0=tmpb[:, 0:1], scalar=-1.0, in1=tmpa[:, 0:1],
                                        op0=ALU.add, op1=ALU.mult))
            V.scalar_tensor_tensor(out=gbf, in0=tmpb[:, 1:2], scalar=-1.0, in1=tmpa[:, 1:2],
                                   op0=ALU.add, op1=ALU.mult).then_inc(v_mod, 1)
            dve.wait_ge(s_wl, 112)
            for j in range(4):
                dve.wait_ge(t_v, j + 1)
                V.tensor_tensor(vtok[:, 512 * j:512 * j + 512].rearrange("p (t d) -> p t d", t=4),
                                ps[:, 512 * j:512 * j + 512].rearrange("p (t d) -> p t d", t=4),
                                bvr[:, None, :].broadcast_to([P, 4, P]), ALU.add).then_inc(v_v, 1)
            for s in range(NT):
                base = T * (s % 2)
                dve.wait_ge(t_s, s + 1)
                d = ps[:, base + P * s:base + P * s + P]
                link(V.tensor_tensor(d, d, diag[:, :], ALU.add))
                link(V.tensor_reduce(mx[:, s:s + 1], ps[:, base + P * s:base + T], AX.X, ALU.max))
                V.tensor_scalar(negm[:, s:s + 1], mx[:, s:s + 1], -SCALE, None, ALU.mult).then_inc(v_nm, 1)
            V.tensor_reduce(mcol, mx, AX.X, ALU.max).then_inc(v_mrow, 1)
            dve.wait_ge(t_mr, 1)
            V.tensor_reduce(mrow[0:1, 0:1], ps[0:1, 0:P], AX.X, ALU.max).then_inc(v_mrow, 1)
            dve.wait_ge(t_mc, 1)
            V.tensor_scalar(mcol, ps[:, 512:513], -SCALE, None, ALU.mult).then_inc(v_mcol, 1)
            dve.wait_ge(a_gs, 1)
            dve.wait_ge(a_e, NT)
            link(V.tensor_tensor(esum, esum, gs, ALU.mult))
            V.tensor_reduce(zc, esum, AX.X, ALU.add).then_inc(v_z, 1)
            dve.wait_ge(t_z, 1)
            link(V.reciprocal(zr, ps[:, 1024:1025]))
            link(V.tensor_scalar(gs, gs, zr, None, ALU.mult))
            v3 = vtok[:, :].rearrange("p (t d) -> p t d", t=NT)
            V.tensor_tensor(v3, v3, gs[:, :, None].broadcast_to([P, NT, P]), ALU.mult).then_inc(v_vs, 1)
            for j in range(4):
                dve.wait_ge(t_av, j + 1)
                d = x1[:, 512 * j:512 * j + 512]
                V.scalar_tensor_tensor(out=d, in0=ps[:, 512 * j:512 * j + 512], scalar=gaf, in1=d,
                                       op0=ALU.mult, op1=ALU.add).then_inc(v_x1, 1)
                dve.wait_ge(t_x1t, j + 1)
                tiles = range(4 * j, 4 * j + 4)
                layer_stats(lambda t: ps[:, T + P * t:T + P * t + P], tiles)
                for t in tiles:
                    V.tensor_scalar(xntok[:, t, :], ps[:, T + P * t:T + P * t + P], bnmv[:, 2 * t:2 * t + 1],
                                    rs16[:, t:t + 1], ALU.subtract, ALU.mult).then_inc(v_xn2, 1)

            CH = 14
            start = chained[0]

            def heads(ap):
                return ap.rearrange("p (h w d) -> p h w d", h=H, w=2)

            def rot(ap):
                return heads(ap)[:, :, ::-1, :]

            def table(u, k):
                return tabs[u][:, DH * k:DH * k + DH].rearrange("p (w d) -> p w d", w=2)[:, None, :, :]\
                    .broadcast_to([P, H, 2, DH // 2])

            def step(n, u):
                count = [0]

                def linked():
                    dve.wait_ge(v_ch, n * CH + (start + count[0]))

                def link_on(times=1):
                    for _ in range(times):
                        if count[0] > 0:
                            linked()
                        chain[count[0]]().then_inc(v_ch, 1)
                        count[0] += 1

                a_, b_, y_, x_ = nw_a[:, 0:33], nw_b[:, 0:33], nw_y[:, 0:33], nw_x[:, 0:33]
                chain = [
                    lambda: V.bn_aggr(mv2, st2) if live(n - 3) else V.memset(mv2, 0.0),
                    lambda: V.tensor_scalar(nw_x[:, 32:33], mv2[:, 1:2], LN_EPS, None, ALU.add),
                    lambda: V.tensor_scalar(nw_x[:, 0:32], nw_x[:, 0:32], NORM_EPS2, None, ALU.max)
                    if live(n) else V.memset(nw_x[:, 0:32], 1.0),
                    lambda: V.tensor_scalar(a_.bitcast(I32), x_.bitcast(I32), 1, None, ALU.logical_shift_right),
                    lambda: V.tensor_scalar(y_.bitcast(I32), a_.bitcast(I32), -1.0, float(MAGIC),
                                            ALU.mult, ALU.add),
                ]
                for k in range(3):
                    chain += [
                        lambda: V.tensor_tensor(a_, x_, y_, ALU.mult),
                        lambda: V.scalar_tensor_tensor(out=b_, in0=a_, scalar=-0.5, in1=y_,
                                                       op0=ALU.mult, op1=ALU.mult),
                        lambda k=k: V.scalar_tensor_tensor(out=rk[u] if k == 2 else y_, in0=b_, scalar=1.5,
                                                           in1=y_, op0=ALU.add, op1=ALU.mult),
                    ]
                assert len(chain) == CH
                chained_step = live(n) or live(n - 3)

                if live(n - 2):
                    need(dve, "a_ex", n - 2)
                    need(dve, "g_pn", n - 3)
                    V.tensor_reduce(rsum, pr.rearrange("p (h k) -> p h k", h=H), AX.X, ALU.add)\
                        .then_inc(S["v_sum"], 1)
                    need(dve, "v_sum", n - 2)
                    V.reciprocal(ri_, rsum).then_inc(S["v_ri"], 1)
                if live(n):
                    need(dve, "t_pq", n)
                    need(dve, "g_tab", n)
                    need(dve, "t_tq", n - 1)
                    V.tensor_tensor(heads(qc), heads(pj), table(u, 0), ALU.mult)
                if live(n):
                    V.tensor_tensor(heads(qsn), rot(pj), table(u, 1), ALU.mult).then_inc(S["v_qq"], 1)
                if live(n - 5):
                    need(dve, "t_tf", n - 5)
                    need(dve, "a_xs", n - 4)
                    t5 = tile_of(n - 5)
                    V.scalar_tensor_tensor(out=xa[:, bass.ds(t5 * P + PAD, P)], in0=b6[:, 0:P],
                                           scalar=b2T[:, bass.ds(layer_of(n - 5), 1)],
                                           in1=xb[:, bass.ds(t5 * P + 1, P)], op0=ALU.add, op1=ALU.add)\
                        .then_inc(S["v_xa"], 1)
                if live(n - 3):
                    need(dve, "t_to", n - 3)
                    t3 = tile_of(n - 3)
                    V.tensor_tensor(xb[:, bass.ds(t3 * P + 1, P)], b7[:, 0:P], xa[:, bass.ds(t3 * P + PAD, P)],
                                    ALU.add).then_inc(S["v_xb"], 1)
                if live(n):
                    need(dve, "a_sqq", n)
                    V.tensor_reduce(nw_x[:, 0:16], sqq.rearrange("p (h d) -> p h d", h=H), AX.X, ALU.add)\
                        .then_inc(S["v_ssq"], 1)
                if live(n):
                    need(dve, "t_pk", n)
                    need(dve, "t_tk", n - 1)
                    V.tensor_tensor(heads(kc), heads(pj), table(u, 2), ALU.mult)
                if live(n):
                    V.tensor_tensor(heads(ksn), rot(pj), table(u, 3), ALU.mult).then_inc(S["v_kk"], 1)
                if live(n - 1):
                    need(dve, "t_sc", n - 1)
                    need(dve, "a_ex", n - 2)
                    V.tensor_tensor(sm.rearrange("p (a r k) -> p r a k", r=2, k=NK),
                                    sy.rearrange("p (r a k) -> p r a k", r=2, k=NK),
                                    maskb[:, bass.ds(tile_of(n - 1) * NK, NK)][:, None, None, :]
                                    .broadcast_to([P, 2, PR, NK]), ALU.add).then_inc(S["v_ms"], 1)
                if live(n - 4):
                    need(dve, "t_hg", n - 4)
                    need(dve, "a_gel", n - 5)
                    dve.wait_ge(s_b1, (layer_of(n - 4) + 1) * 16)
                    V.tensor_tensor(gate, b6[:, 0:FI], b1b[:, bass.ds(slot_of(n - 4) * 2 * FI + FI, FI)],
                                    ALU.add).then_inc(S["v_gate"], 1)
                if live(n - 3):
                    need(dve, "t_x2", n - 3)
                    V.tensor_copy(x2c, b7[:, 2 * P:3 * P])
                    V.bn_stats(st2, b7[:, 2 * P:3 * P]).then_inc(S["v_bn"], 1)
                if live(n - 1):
                    need(dve, "v_ms", n - 1)
                    need(dve, "g_sub", n - 2)
                    V.tensor_reduce(smax, sm.rearrange("p (h k) -> p h k", h=H), AX.X, ALU.max)\
                        .then_inc(S["v_mx"], 1)
                if live(n - 4):
                    need(dve, "t_ha", n - 4)
                    need(dve, "g_h", n - 5)
                    V.tensor_tensor(ha, b6[:, 0:FI], b1b[:, bass.ds(slot_of(n - 4) * 2 * FI, FI)],
                                    ALU.add).then_inc(S["v_ha"], 1)
                if live(n):
                    need(dve, "a_sqk", n)
                    V.tensor_reduce(nw_x[:, 16:32], sqk.rearrange("p (h d) -> p h d", h=H), AX.X, ALU.add)\
                        .then_inc(S["v_ssk"], 1)
                if chained_step:
                    apart(dve)
                    need(dve, "v_bn", n - 3)
                    need(dve, "v_ssk", n)
                    need(dve, "v_ssq", n)
                    need(dve, "g_krn", n - 2)
                    link_on(CH)
                    linked()
                if live(n):
                    need(dve, "g_sq", n - 2)
                    V.tensor_scalar(q8[u], rk[u][:, 0:16], 8.0, None, ALU.mult).then_inc(S["v_rs"], 1)
                if live(n - 3):
                    need(dve, "t_xnt", n - 4)
                    V.tensor_scalar(xn2, x2c, mv2[:, 0:1], rk[u][:, 32:33], ALU.subtract, ALU.mult)\
                        .then_inc(S["v_lnx"], 1)

            dve.wait_ge(s_lnp, 64)
            dve.wait_ge(s_msk, 16)
            dve.wait_ge(a_xa, 4)
            V.memset(mv2, 0.0).then_inc(S["v_xa"], NT)
            run(dve, step)

            need(dve, "v_xa", E - 1)
            for i in range(4):
                d = x1[:, 512 * i:512 * i + 512]
                V.scalar_tensor_tensor(out=d, in0=xa[:, PAD + 512 * i:PAD + 512 * i + 512], scalar=gbf, in1=d,
                                       op0=ALU.mult, op1=ALU.add).then_inc(v_fin, 1)

        @block.gpsimd
        def _(pool):
            G = nc.gpsimd
            pool.wait_ge(t_av, 4)
            G.memset(xa[:, 0:PAD], 0.0).then_inc(g_init, 1)
            G.memset(xb[:, 0:1], 0.0).then_inc(g_init, 1)
            G.memset(KT, 0.0).then_inc(g_init, 1)

            def scaled_tables(e, u):
                need(pool, "v_kk", e - 2)
                pool.wait_ge(s_scl, (layer_of(e) + 1) * 96)
                G.tensor_tensor(tabs[u], tabb[:, bass.ds(tile_of(e) * 4 * DH, 4 * DH)],
                                scl[:, bass.ds(slot_of(e) * 4 * DH, 4 * DH)], ALU.mult).then_inc(S["g_tab"], 1)

            def step(n, u):
                if live(n - 2):
                    need(pool, "v_ri", n - 2)
                    p3 = pr.rearrange("p (h k) -> p h k", h=H)
                    G.tensor_tensor(p3, p3, ri_[:, :, None].broadcast_to([P, H, NK]), ALU.mult)\
                        .then_inc(S["g_pn"], 1)
                if live(n + 1):
                    scaled_tables(n + 1, 1 - u)
                if live(n):
                    need(pool, "v_qq", n)
                    G.tensor_tensor(qc, qc, qsn, ALU.add).then_inc(S["g_qr"], 1)
                if live(n):
                    need(pool, "v_kk", n)
                    G.tensor_tensor(kc, kc, ksn, ALU.add).then_inc(S["g_kr"], 1)
                if live(n - 1):
                    need(pool, "v_mx", n - 1)
                    s3 = sm.rearrange("p (h k) -> p h k", h=H)
                    G.tensor_tensor(s3, s3, smax[:, :, None].broadcast_to([P, H, NK]), ALU.subtract)\
                        .then_inc(S["g_sub"], 1)
                if live(n - 4):
                    need(pool, "v_ha", n - 4)
                    need(pool, "a_gel", n - 4)
                    need(pool, "t_th", n - 5)
                    G.tensor_tensor(hh, ha, gel, ALU.mult).then_inc(S["g_h"], 1)
                if live(n - 1):
                    need(pool, "g_sub", n - 1)
                    need(pool, "v_rs", n - 1)
                    s3 = sm.rearrange("p (h k) -> p h k", h=H)
                    G.tensor_tensor(s3, s3, q8[1 - u][:, :, None].broadcast_to([P, H, NK]), ALU.mult)\
                        .then_inc(S["g_sq"], 1)
                if live(n):
                    need(pool, "v_rs", n)
                    need(pool, "g_kr", n)
                    k3 = kc.rearrange("p (h d) -> p h d", h=H)
                    G.tensor_tensor(k3, k3, rk[u][:, 16:32][:, :, None].broadcast_to([P, H, DH]), ALU.mult)\
                        .then_inc(S["g_krn"], 1)

            pool.wait_ge(a_xa, 4)
            pool.wait_ge(s_tab, 16)
            pool.wait_ge(s_lnp, 64)
            pool.wait_ge(g_init, 3)
            scaled_tables(0, 0)
            run(pool, step, E - UNROLL)


_INS = ["L0_attn_x", "L0_attn_Wq", "L0_attn_bq", "L0_attn_Wk", "L0_attn_bk", "L0_attn_Wv", "L0_attn_bv",
        "L0_ffn_Wqkv", "L0_ffn_q_scale", "L0_ffn_k_scale", "L0_ffn_Wo", "L0_ffn_ln_g", "L0_ffn_ln_b",
        "L0_ffn_W1", "L0_ffn_b1", "L0_ffn_W2", "L0_ffn_b2", "L0_c", "L0_wmod"]


def kernel(**inputs):
    import concourse.bacc as bacc
    from concourse.bass_utils import run_bass_kernel_spmd

    nc = bacc.Bacc("TRN2", target_bir_lowering=False, num_devices=1)
    by_channel = ("L0_ffn_ln_g", "L0_ffn_ln_b", "L0_ffn_b2", "L0_c")
    arrays = {"in_" + n: np.ascontiguousarray(inputs[n].T if n in by_channel else inputs[n]) for n in _INS}
    for n, a in zip(("eye", "rotary", "mask", "diagonal", "carry"), shape_tables()):
        arrays["const_" + n] = a
    aps = [nc.dram_tensor(n, a.shape, mybir.dt.from_np(a.dtype), kind="ExternalInput").ap()
           for n, a in arrays.items()]
    out = nc.dram_tensor("out", (1, T, P), F32, kind="ExternalOutput").ap()
    program(nc, *aps, out)
    r = run_bass_kernel_spmd(nc, [arrays], core_ids=[0])
    return r.results[0]["out"]
```
